# Optimizing a Trainium2 kernel written in Bass

```python
import numpy as np
import jax
import jax.numpy as jnp

def _softmax(x, axis=-1):
    return jax.nn.softmax(x, axis=axis)

def _gelu(x):
    return jax.nn.gelu(x, approximate=True)

def _silu(x):
    return jax.nn.silu(x)

def _sigmoid(x):
    return jax.nn.sigmoid(x)

def _layernorm(x, axis=-1, eps=1e-05):
    m = jnp.mean(x, axis=axis, keepdims=True)
    v = jnp.var(x, axis=axis, keepdims=True)
    return (x - m) / jnp.sqrt(v + eps)

def _scatter_add(tgt, idx, src, axis=0):
    return tgt.at[idx].add(src)

def _segment_sum(src, seg, n):
    return jax.ops.segment_sum(src, seg, n)
kernel_name = 'mk_xattn_ffn_d1_seqx_r4_8b076a'

def setup_inputs(seed: int=0):
    np.random.seed(seed)
    _w = jnp.asarray

    def _rec_inputs():
        import jax
        import jax.numpy as jnp
        _rk = jax.random.key(seed)
        x = 7.22e-05 + 1 * jax.random.normal(jax.random.fold_in(_rk, 1), (4, 512, 256), jnp.float32)
        _lenS = 512 - jax.random.randint(jax.random.fold_in(_rk, 7), (4,), 0, max(1, 512 // 4) + 1, jnp.int32)
        _lenS2 = 512 - jax.random.randint(jax.random.fold_in(_rk, 8), (4,), 0, max(1, 512 // 4) + 1, jnp.int32)
        _ctx_1024P = jax.random.normal(jax.random.fold_in(_rk, 11), (4, 16, 256), jnp.float32)
        _ctx_1024c = jax.random.dirichlet(jax.random.fold_in(_rk, 511), 0.3 * jnp.ones((16,), jnp.float32), (4, 512))
        _ctx_1024t = jnp.einsum('bsk,bkd->bsd', _ctx_1024c, _ctx_1024P)
        _ctx_1024t = _ctx_1024t * jax.lax.rsqrt(jnp.mean(jnp.square(_ctx_1024t)) + 1e-12) * 0.953939
        ctx_1024 = 4.13588e-05 + 0.999923 * (_ctx_1024t + 0.3 * jax.random.normal(jax.random.fold_in(_rk, 611), (4, 512, 256), jnp.float32))
        return (x, ctx_1024)
    x, ctx_1024 = _rec_inputs()

    def _L0_xattn_setup():
        import jax, jax.numpy as jnp
        import numpy as np
        B, T, D, H = (4, 512, 256, 1024)
        S = 64
        EPS = 1e-05

        def _layer_norm(x, gamma, beta):
            mu = jnp.mean(x, axis=-1, keepdims=True)
            var = jnp.mean(jnp.square(x - mu), axis=-1, keepdims=True)
            return (x - mu) * jax.lax.rsqrt(var + EPS) * gamma + beta

        def _aft_local(emb, wq, bq, wk, bk, wv, bv, wo, bo, pos_bias):
            q = emb @ wq + bq
            k = emb @ wk + bk
            v = emb @ wv + bv
            idx = jnp.arange(T)
            mask = (jnp.abs(idx[:, None] - idx[None, :]) < S).astype(pos_bias.dtype)
            w = pos_bias * mask
            max_k = jnp.max(k, axis=1, keepdims=True)
            max_w = jnp.max(w, axis=1, keepdims=True)
            ek = jnp.exp(k - max_k)
            ew = jnp.exp(w - max_w)
            num = jnp.einsum('tj,bjd->btd', ew, ek * v)
            den = jnp.einsum('tj,bjd->btd', ew, ek)
            y = jax.nn.sigmoid(q) * num / den
            return y @ wo + bo
        key = jax.random.key(seed)
        ks = jax.random.split(key, 16)
        sd = 0.02
        return {'x': jax.random.normal(ks[0], (B, T, D), jnp.float32), 'pos_encod': jax.random.normal(ks[1], (B, T, D), jnp.float32), 'wq': jax.random.normal(ks[2], (D, D), jnp.float32) * sd, 'bq': jnp.zeros((D,), jnp.float32), 'wk': jax.random.normal(ks[3], (D, D), jnp.float32) * sd, 'bk': jnp.zeros((D,), jnp.float32), 'wv': jax.random.normal(ks[4], (D, D), jnp.float32) * sd, 'bv': jnp.zeros((D,), jnp.float32), 'wo': jax.random.normal(ks[5], (D, D), jnp.float32) * sd, 'bo': jnp.zeros((D,), jnp.float32), 'pos_bias': jax.random.normal(ks[6], (T, T), jnp.float32) * sd, 'gamma': jnp.ones((D,), jnp.float32), 'beta': jnp.zeros((D,), jnp.float32), 'w1': jax.random.normal(ks[7], (D, H), jnp.float32) * sd, 'b1': jnp.zeros((H,), jnp.float32), 'w2': jax.random.normal(ks[8], (H, D), jnp.float32) * sd, 'b2': jnp.zeros((D,), jnp.float32)}
    _L0_xattn_all = _L0_xattn_setup()
    _L0_xattn_in = {k: v for k, v in _L0_xattn_all.items() if k in ('wq', 'bq', 'wk', 'bk', 'wv', 'bv', 'wo', 'bo', 'pos_bias', 'gamma', 'beta', 'w1', 'b1', 'w2', 'b2')}
    del _L0_xattn_all

    def _L0_ffn_setup():
        import jax, jax.numpy as jnp
        import numpy as np
        B, M, D = (4, 512, 256)
        N, P = (64, 32)
        key = jax.random.key(seed)
        k1, k2, k3, k4 = jax.random.split(key, 4)
        x = jax.random.normal(k1, (B, M, D), dtype=jnp.float32)
        phi = jax.random.normal(k2, (D, N, P), dtype=jnp.float32) * (1.0 / np.sqrt(D))
        W = jax.random.normal(k3, (N, D, D), dtype=jnp.float32) * (1.0 / np.sqrt(D))
        b = jax.random.normal(k4, (N, D), dtype=jnp.float32) * 0.01
        return {'x': x, 'phi': phi, 'W': W, 'b': b}
    _L0_ffn_all = _L0_ffn_setup()
    _L0_ffn_in = {k: v for k, v in _L0_ffn_all.items() if k in ('phi', 'W', 'b')}
    del _L0_ffn_all
    return {'x': x, 'ctx_1024': ctx_1024, 'L0_xattn_wq': _L0_xattn_in['wq'], 'L0_xattn_bq': _L0_xattn_in['bq'], 'L0_xattn_wk': _L0_xattn_in['wk'], 'L0_xattn_bk': _L0_xattn_in['bk'], 'L0_xattn_wv': _L0_xattn_in['wv'], 'L0_xattn_bv': _L0_xattn_in['bv'], 'L0_xattn_wo': _L0_xattn_in['wo'], 'L0_xattn_bo': _L0_xattn_in['bo'], 'L0_xattn_pos_bias': _L0_xattn_in['pos_bias'], 'L0_xattn_gamma': _L0_xattn_in['gamma'], 'L0_xattn_beta': _L0_xattn_in['beta'], 'L0_xattn_w1': _L0_xattn_in['w1'], 'L0_xattn_b1': _L0_xattn_in['b1'], 'L0_xattn_w2': _L0_xattn_in['w2'], 'L0_xattn_b2': _L0_xattn_in['b2'], 'L0_ffn_phi': _L0_ffn_in['phi'], 'L0_ffn_W': _L0_ffn_in['W'], 'L0_ffn_b': _L0_ffn_in['b']}

def reference(x, ctx_1024, L0_xattn_wq, L0_xattn_bq, L0_xattn_wk, L0_xattn_bk, L0_xattn_wv, L0_xattn_bv, L0_xattn_wo, L0_xattn_bo, L0_xattn_pos_bias, L0_xattn_gamma, L0_xattn_beta, L0_xattn_w1, L0_xattn_b1, L0_xattn_w2, L0_xattn_b2, L0_ffn_phi, L0_ffn_W, L0_ffn_b):
    import jax
    import jax.numpy as jnp

    def _L0_xattn_ref(x, pos_encod, wq, bq, wk, bk, wv, bv, wo, bo, pos_bias, gamma, beta, w1, b1, w2, b2):
        import jax, jax.numpy as jnp
        import numpy as np
        B, T, D, H = (4, 512, 256, 1024)
        S = 64
        EPS = 1e-05

        def _layer_norm(x, gamma, beta):
            mu = jnp.mean(x, axis=-1, keepdims=True)
            var = jnp.mean(jnp.square(x - mu), axis=-1, keepdims=True)
            return (x - mu) * jax.lax.rsqrt(var + EPS) * gamma + beta

        def _aft_local(emb, wq, bq, wk, bk, wv, bv, wo, bo, pos_bias):
            q = emb @ wq + bq
            k = emb @ wk + bk
            v = emb @ wv + bv
            idx = jnp.arange(T)
            mask = (jnp.abs(idx[:, None] - idx[None, :]) < S).astype(pos_bias.dtype)
            w = pos_bias * mask
            max_k = jnp.max(k, axis=1, keepdims=True)
            max_w = jnp.max(w, axis=1, keepdims=True)
            ek = jnp.exp(k - max_k)
            ew = jnp.exp(w - max_w)
            num = jnp.einsum('tj,bjd->btd', ew, ek * v)
            den = jnp.einsum('tj,bjd->btd', ew, ek)
            y = jax.nn.sigmoid(q) * num / den
            return y @ wo + bo
        emb = x + pos_encod
        attn = _aft_local(emb, wq, bq, wk, bk, wv, bv, wo, bo, pos_bias)
        a = _layer_norm(attn + emb, gamma, beta)
        ff = jax.nn.relu(a @ w1 + b1) @ w2 + b2
        return _layer_norm(ff + a, gamma, beta)

    def _L0_ffn_ref(x, phi, W, b):
        import jax, jax.numpy as jnp
        import numpy as np
        B, M, D = (4, 512, 256)
        N, P = (64, 32)
        logits = jnp.einsum('bmd,dnp->bmnp', x, phi)
        dispatch = jax.nn.softmax(logits, axis=0)
        bsz, m, n, p = logits.shape
        combine = jax.nn.softmax(logits.reshape(bsz, m, n * p), axis=-1).reshape(bsz, m, n, p)
        slots = jnp.einsum('bmd,bmnp->bnpd', x, dispatch)
        y = jnp.einsum('bnpd,nde->bnpe', slots, W) + b[None, :, None, :]
        out = jnp.einsum('bnpd,bmnp->bmd', y, combine)
        return out
    x = x + _L0_xattn_ref(_layernorm(x, axis=-1), ctx_1024, L0_xattn_wq, L0_xattn_bq, L0_xattn_wk, L0_xattn_bk, L0_xattn_wv, L0_xattn_bv, L0_xattn_wo, L0_xattn_bo, L0_xattn_pos_bias, L0_xattn_gamma, L0_xattn_beta, L0_xattn_w1, L0_xattn_b1, L0_xattn_w2, L0_xattn_b2)
    x = x + _L0_ffn_ref(_layernorm(x, axis=-1), L0_ffn_phi, L0_ffn_W, L0_ffn_b)
    return x

_drawn_inputs = setup_inputs


def setup_inputs(seed=0):
    import zlib

    import numpy as np

    out = dict(_drawn_inputs(seed))
    spreads = {'L0_xattn_bq': (0.0, 2.0),
     'L0_xattn_bk': (0.0, 2.0),
     'L0_xattn_bv': (0.0, 0.32),
     'L0_xattn_bo': (0.0, 0.1),
     'L0_xattn_gamma': (1.0, 0.2),
     'L0_xattn_beta': (0.0, 0.1),
     'L0_xattn_b1': (0.0, 0.1),
     'L0_xattn_b2': (0.0, 0.1)}
    factors = {'L0_xattn_wq': 8.0, 'L0_xattn_wk': 8.0, 'L0_xattn_pos_bias': 200.0, 'L0_ffn_b': 200.0}
    for name, (base, spread) in spreads.items():
        noise = np.random.default_rng([zlib.crc32(name.encode()), seed]).standard_normal(out[name].shape)
        drawn = base * np.exp(spread * noise) if base else spread * noise
        out[name] = jnp.asarray(drawn.astype(out[name].dtype))
    for name, factor in factors.items():
        out[name] = (out[name] * factor).astype(out[name].dtype)
    return out
```

```python
from contextlib import ExitStack

import concourse.bass as bass
from concourse import mybir

F32 = mybir.dt.float32
F32R = mybir.dt.float32r
F16 = mybir.dt.float16
ALU = mybir.AluOpType
ACT = mybir.ActivationFunctionType
AX_X = mybir.AxisListType.X


def reached(n, first=1):
    return not isinstance(n, int) or n >= first


class Order:

    def __init__(self, base):
        self.base, self.k = base, 0

    def step(self):
        self.k += 1
        return self.k

    def value(self, k):
        return self.base + k


def bass_aft_soft_moe(nc, x, ctx_in, wq, bq, wk, bk, wv, bv, wo, bo, pos_bias, gamma, beta,
                      w1, b1, w2, b2, phi, W, eb, out):
    P = 128
    B, T, D = x.shape
    H = w1.shape[1]
    NE, _, PE_ = phi.shape[1], phi.shape[0], phi.shape[2]
    NS = NE * PE_
    TT = T // P
    DH = D // P
    HT = H // P
    CE = 8
    CS = CE * PE_
    CH = NE // CE
    SUB = CS // P
    EPS = 1e-5
    BAND = 64
    Z_SCALE = 256.0
    D_SCALE = 4096.0
    LOWEST = -3.0e38
    QKV = 3 * DH
    SUMS_BANKS = ((2, 3), (0, 1))
    STEPS_A0, STEPS_A, STEPS_A1, STEPS_B = 32, 57, 39, 36
    assert B * PE_ == P and SUB == 2 and DH == 2 and TT == 4

    x_d = x.rearrange("b (t p) d -> b p t d", p=P)
    ctx_d = ctx_in.rearrange("b (t p) d -> b p t d", p=P)
    out_d = out.rearrange("b (t p) d -> b p t d", p=P)
    phi_d = phi.rearrange("(h p) (c n) s -> c p h (n s)", p=P, n=CE)
    eb_d = eb.rearrange("(c n) e -> c (n e)", n=CE)
    W_d = W.rearrange("(c n) (h p) e -> c p n h e", p=P, n=CE)
    spill = nc.dram_tensor("x1_spill", (B, T, D), F32, kind="Internal").ap()
    spill_d = spill.rearrange("b (t p) d -> b p t d", p=P)

    with ExitStack() as stack:
        def sb(name, shape, dt, where=stack):
            return where.enter_context(nc.sbuf_tensor(name, shape, dt))

        logits_ps = [stack.enter_context(nc.psum_tensor(f"ps_pair{i}", [P, B, CS], F32))[:, :, :] for i in range(2)]
        psum = [logits_ps[k // 2][:, 2 * (k % 2):2 * (k % 2) + 2, :].rearrange("p a n -> p (a n)") for k in range(4)]
        psum += [stack.enter_context(nc.psum_tensor(f"ps{k}", [P, 512], F32))[:, :] for k in range(4, 8)]

        ident = sb("ident", [P, P], F32)
        zTh = sb("zTh", [P, DH, B, T], F32R)
        zTl = sb("zTl", [P, DH, B, T], F32R)
        z16h = sb("z16h", [P, B, TT, D], F16)
        z16l = sb("z16l", [P, B, TT, D], F16)

        stage_a = ExitStack()
        xf = sb("xf", [P, TT, D], F32, stage_a)
        ctxf = sb("ctxf", [P, TT, D], F32, stage_a)
        emb = sb("emb", [P, TT, D], F32, stage_a)
        embb = sb("embb", [P, TT, D], F32, stage_a)
        embTh = sb("embTh", [P, DH, T], F32R, stage_a)
        embTl = sb("embTl", [P, DH, T], F32R, stage_a)
        wqkvh = sb("wqkvh", [P, 3, DH, D], F32R, stage_a)
        wqkvl = sb("wqkvl", [P, 3, DH, D], F32R, stage_a)
        wo_sb = sb("wo_sb", [P, DH, D], F32, stage_a)
        w1h = sb("w1h", [P, DH, H], F32R, stage_a)
        w1l = sb("w1l", [P, DH, H], F32R, stage_a)
        w2_sb = sb("w2_sb", [P, HT, D], F32, stage_a)
        ewTh = sb("ewTh", [P, TT, T], F32R, stage_a)
        ewTl = sb("ewTl", [P, TT, T], F32R, stage_a)
        rows = sb("rows", [P, 4, D], F32, stage_a)
        cols = sb("cols", [P, 3, DH], F32, stage_a)
        nbq = sb("nbq", [P, DH], F32, stage_a)
        b1c = sb("b1c", [P, HT], F32, stage_a)
        km = sb("km", [P, DH], F32, stage_a)
        kmb = sb("kmb", [P, DH], F32, stage_a)
        kb = sb("kb", [P, DH], F32, stage_a)
        wmax = sb("wmax", [P, TT], F32, stage_a)
        nwmax = sb("nwmax", [P, TT], F32, stage_a)
        mhalf = sb("mhalf", [P, TT], F32, stage_a)
        LN = ("x", "a", "f", "z")
        st = {n: sb(f"st_{n}", [P, TT, 6], F32, stage_a) for n in LN}
        mv = {n: sb(f"mv_{n}", [P, TT, 2], F32, stage_a) for n in LN}
        ve = {n: sb(f"ve_{n}", [P, TT], F32, stage_a) for n in LN}
        rstd = {n: sb(f"rstd_{n}", [P, TT], F32, stage_a) for n in LN}
        setup = ExitStack()
        pos = sb("pos", [P, TT, T], F32, setup)
        wqkv_raw = sb("wqkv_raw", [P, 3, DH, D], F32, setup)
        w1_raw = sb("w1_raw", [P, DH, H], F32, setup)
        setup.close()
        hT = sb("hT", [P, HT, T], F32, stage_a)
        aTh = sb("aTh", [P, DH, T], F32R, stage_a)
        aTl = sb("aTl", [P, DH, T], F32R, stage_a)
        a_sb = sb("a_sb", [P, TT, D], F32, stage_a)
        ab2 = sb("ab2", [P, TT, D], F32, stage_a)
        xb = sb("xb", [P, TT, D], F32, stage_a)
        z_sb = sb("z_sb", [P, TT, D], F32, stage_a)
        eq = sb("eq", [P, DH, T], F32, stage_a)
        ekT = sb("ekT", [P, DH, T], F32, stage_a)
        ekvT = sb("ekvT", [P, DH, T], F32, stage_a)
        EKh = sb("EKh", [P, TT, 2 * D], F32R, stage_a)
        EKl = sb("EKl", [P, TT, 2 * D], F32R, stage_a)
        yT = sb("yT", [P, DH, T], F32, stage_a)
        stage_a.close()

        Wr = sb("Wr", [P, CE, DH, D], F32)
        phi_raw = sb("phi_raw", [P, DH, CS], F32)
        phih = sb("phih", [P, 2, DH, CS], F32R)
        phil = sb("phil", [P, 2, DH, CS], F32R)
        ebb = sb("ebb", [P, CE, D], F32)
        disph = sb("disph", [P, 2, TT, B, CS], F16)
        displ = sb("displ", [P, 2, TT, B, CS], F16)
        e2 = sb("e2", [P, TT, B, CS], F32)
        combT = sb("combT", [P, SUB, B, TT, P], F32)
        slotsT = sb("slotsT", [P, DH, CE, B, PE_], F32)
        y_sb = sb("y_sb", [P, CE, D], F32)
        y_c = sb("y_c", [P, SUB, B, D], F32)
        acc = sb("acc", [P, B, TT, D], F32)
        l0c = sb("l0c", [P, CS], F32)
        mx = sb("mx", [P, CS], F32)
        ed = sb("ed", [P, 2, B, CS], F32)
        s01 = sb("s01", [P, 2, CS], F32)
        ssum = sb("ssum", [P, CS], F32)
        cmax = sb("cmax", [P, TT, B], F32)
        nR = sb("nR", [P, TT, B], F32)
        nRn = sb("nRn", [P, TT, B], F32)
        dR = sb("dR", [P, TT, B], F32)
        alpha = sb("alpha", [P, TT, B], F32)
        alpha_use = sb("alpha_use", [P, TT, B], F32)
        csum = sb("csum", [P, TT, B], F32)
        S = sb("S", [P, TT, B], F32)
        rS = sb("rS", [P, TT, B], F32)

        x1_view = Wr[:].rearrange("p (b t) h e -> p b (t h) e", b=B)

        names = """ident_made consts_made band_masked x_in ctx_arrived xb_in wqkv_in w1_in pos_in vectors_in
            wo_w2_in pool_order dve_order wqkv_hi w1_hi wqkv_lo w1_lo wmax_ready ew_ready ew_T ewT_hi ewT_lo
            nbq_ready emb_ready embb_made emb_T embT_hi embT_lo qkv_done kb_ready ek_ready eq_ready
            ekv_ready ek_T EK_hi EK_lo sums_done den_read y_ready attn_done s_added a_ready a_T aT_hi aT_lo
            ffn1_done h_ready ffn2_done s2_added x1_ready x1_spilled z_ready z_T z16_hi z16_lo zT_hi zT_lo
            phi_in phi_hi phi_lo eb_in l_full l0_copied nmax_ready sub_ready e_ready d_ready disp_hi disp_lo
            e2_ready alpha_ready alpha_kept slots_done slotsT_ready y_done y_ready_b y_moved comb_T combT_ready
            out_done acc_added s_ready rS_ready x1_back out_ready out_stored zeroed""".split()
        sem = {n: stack.enter_context(nc.semaphore(n)) for n in names}
        dve_order = sem["dve_order"]
        var_ready = {n: stack.enter_context(nc.semaphore(f"var_ready_{n}")) for n in LN}
        rstd_ready = {n: stack.enter_context(nc.semaphore(f"rstd_ready_{n}")) for n in LN}
        W_in = [stack.enter_context(nc.semaphore(f"W_in{g}")) for g in range(2)]

        block = stack.enter_context(nc.Block())

        @block.sync
        def _(sp):
            sp.dma_start(xf[:], x_d[0]).then_inc(sem["x_in"], 16)
            sp.dma_start(ctxf[:], ctx_d[0]).then_inc(sem["ctx_arrived"], 16)
            for i, w in enumerate((wq, wk, wv)):
                sp.dma_start(wqkv_raw[:, i], w.rearrange("(h p) e -> p h e", p=P)).then_inc(sem["wqkv_in"], 16)
            for i, v in enumerate((bo, gamma, beta, b2)):
                sp.dma_start(rows[:, i, :], v.rearrange("(a d) -> a d", a=1).broadcast_to([P, D])).then_inc(sem["vectors_in"], 16)
            for i, v in enumerate((bq, bk, bv)):
                sp.dma_start(cols[:, i, :], v.rearrange("(h p) -> p h", p=P), allow_slow_non_contiguous=True).then_inc(sem["vectors_in"], 16)
            sp.dma_start(b1c[:], b1.rearrange("(h p) -> p h", p=P), allow_slow_non_contiguous=True).then_inc(sem["vectors_in"], 16)
            sp.dma_start(pos[:], pos_bias.rearrange("(t p) j -> p t j", p=P)).then_inc(sem["pos_in"], 16)
            sp.dma_start(w1_raw[:], w1.rearrange("(h p) e -> p h e", p=P)).then_inc(sem["w1_in"], 16)
            sp.dma_start(wo_sb[:], wo.rearrange("(h p) e -> p h e", p=P)).then_inc(sem["wo_w2_in"], 16)
            sp.dma_start(w2_sb[:], w2.rearrange("(h p) e -> p h e", p=P)).then_inc(sem["wo_w2_in"], 16)

            def batch(d, b):
                return d[b] if isinstance(b, int) else d[bass.ds(b, 1)].rearrange("a p t d -> (a p) t d")

            def load_front(b, made):
                sp.wait_ge(sem["emb_ready"], made)
                sp.dma_start(xf[:], batch(x_d, b)).then_inc(sem["x_in"], 16)
                sp.dma_start(ctxf[:], batch(ctx_d, b)).then_inc(sem["ctx_arrived"], 16)

            def load_back(j):
                if reached(j):
                    sp.wait_ge(sem["x1_ready"], j)
                sp.dma_start(xb[:], batch(x_d, j)).then_inc(sem["xb_in"], 16)

            def store_back(j):
                sp.wait_ge(sem["x1_ready"], j + 1)
                sp.dma_start(batch(spill_d, j), ab2[:]).then_inc(sem["x1_spilled"], 16)

            load_front(1, 1)
            sp.wait_ge(sem["w1_lo"], 1)
            sp.wait_ge(sem["wqkv_lo"], 1)
            sp.wait_ge(sem["ewT_lo"], TT)
            load_back(0)
            with sp.Fori(1, B) as i:
                load_front((i + 1) % B, i + 1)
                store_back(i - 1)
                sp.wait_ge(sem["x1_spilled"], 16 * i)
                load_back(i)
            store_back(B - 1)

            sp.wait_ge(sem["zT_lo"], DH * B)
            sp.wait_ge(sem["x1_spilled"], 16 * B)

            def load_phi(c):
                if reached(c):
                    sp.wait_ge(sem["phi_lo"], c)
                src = phi_d[c] if isinstance(c, int) else phi_d[bass.ds(c, 1)].rearrange("a p h s -> (a p) h s")
                sp.dma_start(phi_raw[:], src).then_inc(sem["phi_in"], 16)

            def load_experts(c):
                src = W_d[c] if isinstance(c, int) else W_d[bass.ds(c, 1)].rearrange("a p n h e -> (a p) n h e")
                for g in range(2):
                    if reached(c):
                        sp.wait_ge(sem["y_done"], (CE // 2) * (c - 1) + 2 * g + 2)
                    sp.dma_start(Wr[:, 4 * g:4 * g + 4], src[:, 4 * g:4 * g + 4]).then_inc(W_in[g], 16)
                bias = eb_d[c:c + 1] if isinstance(c, int) else eb_d[bass.ds(c, 1)]
                if reached(c):
                    sp.wait_ge(sem["out_done"], 2 * TT * c)
                sp.dma_start(ebb[:].rearrange("p n e -> p (n e)"), bias.broadcast_to([P, CE * D])).then_inc(sem["eb_in"], 16)

            def move_y(c):
                for n in range(CE):
                    if n % 2 == 0:
                        sp.wait_ge(sem["y_ready_b"], (CE // 2) * c + n // 2 + 1)
                    p0 = PE_ * (n % 4)
                    for b in range(B):
                        sp.dma_start(y_c[p0:p0 + PE_, n // 4, b, :],
                                     y_sb[PE_ * b:PE_ * (b + 1), n, :]).then_inc(sem["y_moved"], 16)

            load_phi(0)
            load_experts(0)
            load_phi(1)
            move_y(0)
            with sp.Fori(1, CH - 1) as c:
                load_phi(c + 1)
                load_experts(c)
                move_y(c)
            load_experts(CH - 1)
            move_y(CH - 1)
            sp.wait_ge(sem["y_done"], (CE // 2) * CH)
            for b in range(B):
                sp.dma_start(x1_view[:, b], spill_d[b]).then_inc(sem["x1_back"], 16)
            for b in range(B):
                sp.wait_ge(sem["out_ready"], TT * (b + 1))
                sp.dma_start(out_d[b], acc[:, b]).then_inc(sem["out_stored"], 16)
            sp.wait_ge(sem["out_stored"], 16 * B)

        @block.gpsimd
        def _(pool):
            pool.memset(ident[:], 0.0).then_inc(sem["pool_order"], 1)
            pool.wait_ge(sem["pool_order"], 1)
            pool.affine_select(out=ident[:], in_=ident[:], compare_op=ALU.not_equal, fill=1.0, base=0,
                               pattern=[[-1, P]], channel_multiplier=1).then_inc(sem["ident_made"], 1)
            pool.memset(mhalf[:], -0.5).then_inc(sem["consts_made"], 1)
            pool.wait_ge(sem["consts_made"], 1)

            def inverse_deviation(n, count):
                pool.wait_ge(var_ready[n], count)
                pool.tensor_tensor(rstd[n][:], ve[n][:], mhalf[:], ALU.pow).then_inc(rstd_ready[n], 1)

            inverse_deviation("x", 1)
            pool.wait_ge(sem["wqkv_hi"], 1)
            pool.tensor_tensor(wqkvl[:], wqkv_raw[:], wqkvh[:].bitcast(F32), ALU.subtract).then_inc(sem["wqkv_lo"], 1)
            pool.wait_ge(sem["pos_in"], 16)
            pool.affine_select(out=pos[:], in_=pos[:], compare_op=ALU.is_ge, fill=0.0, base=BAND - 1,
                               pattern=[[P, TT], [-1, T]], channel_multiplier=1).then_inc(sem["pool_order"], 1)
            pool.wait_ge(sem["pool_order"], 2)
            pool.affine_select(out=pos[:], in_=pos[:], compare_op=ALU.is_ge, fill=0.0, base=BAND - 1,
                               pattern=[[-P, TT], [1, T]], channel_multiplier=-1).then_inc(sem["band_masked"], 1)
            pool.wait_ge(sem["w1_hi"], 1)
            pool.tensor_tensor(w1l[:], w1_raw[:], w1h[:].bitcast(F32), ALU.subtract).then_inc(sem["w1_lo"], 1)

            inverse_deviation("x", 2)
            with pool.Fori(1, B) as i:
                inverse_deviation("a", i)
                inverse_deviation("x", i + 2)
                inverse_deviation("f", i)
                inverse_deviation("z", i)
            for n in ("a", "f", "z"):
                inverse_deviation(n, B)

            def rescale_sums(c):
                for m in range(TT):
                    pool.wait_ge(sem["alpha_ready"], TT * c + m + 1)
                    pool.tensor_tensor(S[:, m], S[:, m], alpha[:, m], ALU.mult).then_inc(sem["pool_order"], 1)
                    pool.wait_ge(sem["pool_order"], TT * c + m + 3)
                    pool.tensor_tensor(S[:, m], S[:, m], csum[:, m], ALU.add).then_inc(sem["s_ready"], 1)

            pool.wait_ge(sem["zeroed"], 3)
            rescale_sums(0)
            with pool.Fori(1, CH) as c:
                pool.wait_ge(sem["s_ready"], TT * c)
                rescale_sums(c)

        @block.scalar
        def _(act):
            def embedding_high(i):
                for h in range(DH):
                    act.wait_ge(sem["emb_T"], DH * i + h + 1)
                    act.activation(embTh[:, h], psum[6 + h], ACT.Copy).then_inc(sem["embT_hi"], 1)

            def exp_kq(i):
                for h in range(DH):
                    act.wait_ge(sem["qkv_done"], QKV * i + h + 1)
                    act.wait_ge(sem["kb_ready"], i + 1)
                    act.activation(ekT[:, h], psum[h], ACT.Exp, bias=kb[:, h:h + 1]).then_inc(sem["ek_ready"], 1)
                for h in range(DH):
                    act.wait_ge(sem["qkv_done"], QKV * i + 2 * DH + h + 1)
                    if reached(i):
                        act.wait_ge(sem["den_read"], DH * i)
                    act.activation(eq[:, h], psum[h], ACT.Exp, bias=nbq[:, h:h + 1], scale=-1.0).then_inc(sem["eq_ready"], 1)

            def exp_w():
                act.wait_ge(sem["wmax_ready"], 1)
                for t in range(TT):
                    act.activation(pos[:, t], pos[:, t], ACT.Exp, bias=nwmax[:, t:t + 1]).then_inc(sem["ew_ready"], 1)
                act.wait_ge(sem["w1_in"], 16)
                act.activation(w1h[:], w1_raw[:], ACT.Copy).then_inc(sem["w1_hi"], 1)
                for j in range(TT):
                    act.wait_ge(sem["ew_T"], j + 1)
                    act.activation(ewTh[:, j], psum[4 + j % 2], ACT.Copy).then_inc(sem["ewT_hi"], 1)

            def ek_high(i):
                for j in range(TT):
                    act.wait_ge(sem["ek_T"], TT * i + j + 1)
                    act.activation(EKh[:, j], psum[6 + j % 2], ACT.Copy).then_inc(sem["EK_hi"], 1)

            def a_high(j):
                for h in range(DH):
                    act.wait_ge(sem["a_T"], DH * j + h + 1)
                    act.activation(aTh[:, h], psum[4 + h], ACT.Copy).then_inc(sem["aT_hi"], 1)

            def hidden(j):
                for m in range(HT):
                    act.wait_ge(sem["ffn1_done"], HT * j + m + 1)
                    act.activation(hT[:, m], psum[4 + m % 2], ACT.Relu,
                                   bias=b1c[:, m:m + 1]).then_inc(sem["h_ready"], 1)

            def z_high(j):
                act.wait_ge(sem["z_ready"], TT * (j + 1))
                act.activation(z16h[:, j], z_sb[:], ACT.Copy, scale=Z_SCALE).then_inc(sem["z16_hi"], 1)
                for h in range(DH):
                    act.wait_ge(sem["z_T"], DH * j + h + 1)
                    act.activation(zTh[:, h, j], psum[4 + h], ACT.Copy).then_inc(sem["zT_hi"], 1)

            act.wait_ge(sem["wqkv_in"], 48)
            act.activation(wqkvh[:], wqkv_raw[:], ACT.Copy).then_inc(sem["wqkv_hi"], 1)
            embedding_high(0)
            act.wait_ge(sem["nbq_ready"], 1)
            exp_kq(0)
            exp_w()
            ek_high(0)
            with act.Fori(1, B) as i:
                embedding_high(i)
                exp_kq(i)
                a_high(i - 1)
                ek_high(i)
                hidden(i - 1)
                z_high(i - 1)
            a_high(B - 1)
            hidden(B - 1)
            z_high(B - 1)

            def phi_high(n):
                act.wait_ge(sem["phi_in"], 16 * (n + 1))
                if reached(n, 2):
                    act.wait_ge(sem["l_full"], TT * (n - 1))
                act.activation(phih[:, n % 2], phi_raw[:], ACT.Copy).then_inc(sem["phi_hi"], 1)

            def dispatch_high(n, m):
                act.wait_ge(sem["d_ready"], TT * n + m + 1)
                if reached(n, 2):
                    act.wait_ge(sem["slots_done"], B * (n - 1))
                act.activation(disph[:, n % 2, m], ed[:, m % 2], ACT.Copy).then_inc(sem["disp_hi"], 1)

            def softmaxes(n, m):
                L = logits_ps[m % 2]
                act.wait_ge(sem["l_full"], TT * n + m + 1)
                if reached(n) or m >= 1:
                    act.wait_ge(sem["nmax_ready"], TT * n + m)
                act.activation(l0c[:], L[:, 0], ACT.Copy).then_inc(sem["l0_copied"], 1)
                if m >= 2:
                    dispatch_high(n, m - 2)
                act.wait_ge(sem["nmax_ready"], TT * n + m + 1)
                act.wait_ge(sem["sub_ready"], TT * n + m + 1)
                if reached(n):
                    act.wait_ge(sem["comb_T"], SUB * (TT * (n - 1) + m + 1))
                if reached(n):
                    act.wait_ge(sem["s_ready"], TT * (n - 1) + m + 1)
                for b in range(B):
                    ins = act.activation(e2[:, m, b], L[:, b], ACT.Exp, bias=nRn[:, m, b:b + 1],
                                         accum_out=csum[:, m, b:b + 1])
                ins.then_inc(sem["e2_ready"], 1)
                if reached(n):
                    act.wait_ge(sem["alpha_kept"], n)
                act.activation(alpha[:, m], dR[:, m], ACT.Exp).then_inc(sem["alpha_ready"], 1)
                act.activation(ed[:, m % 2], ed[:, m % 2], ACT.Exp).then_inc(sem["e_ready"], 1)

            def slots_out(c, b):
                act.wait_ge(sem["slots_done"], B * c + b + 1)
                if reached(c):
                    act.wait_ge(sem["y_done"], (CE // 2) * c)
                act.activation(slotsT[:, :, :, b, :], psum[4 + b % 2].rearrange("p (h n s) -> p h n s", h=DH, n=CE), ACT.Copy,
                               scale=1.0 / (Z_SCALE * D_SCALE)).then_inc(sem["slotsT_ready"], 1)

            def combine_out(n, m):
                for k in range(SUB):
                    act.wait_ge(sem["comb_T"], SUB * (TT * n + m) + k + 1)
                    act.activation(combT[:, k, :, m, :], psum[6 + k].rearrange("p (b t) -> p b t", b=B),
                                   ACT.Copy).then_inc(sem["combT_ready"], 1)

            phi_high(0)
            for m in range(TT):
                softmaxes(0, m)
                combine_out(0, m)
            dispatch_high(0, 2)
            dispatch_high(0, 3)

            def step(c, n=None):
                if n is not None:
                    phi_high(n)
                slots_out(c, 0)
                if n is not None:
                    softmaxes(n, 0)
                slots_out(c, 1)
                slots_out(c, 2)
                if n is not None:
                    softmaxes(n, 1)
                slots_out(c, 3)
                if n is not None:
                    softmaxes(n, 2)
                    softmaxes(n, 3)
                    combine_out(n, 0)
                    dispatch_high(n, 2)
                    combine_out(n, 1)
                    dispatch_high(n, 3)
                    combine_out(n, 2)
                    combine_out(n, 3)

            step(0, 1)
            with act.Fori(1, CH - 1) as c:
                step(c, c + 1)
            step(CH - 1)

        @block.vector
        def _(dve):
            def row(i):
                return rows[:, i:i + 1].broadcast_to([P, TT, D])

            def statistics(n, src, source, count, per_tile=0):
                for t in range(TT):
                    if t == 0 or per_tile:
                        dve.wait_ge(source, count + per_tile * t)
                    dve.bn_stats(st[n][:, t], src[:, t]).then_inc(dve_order, 1)
                    k = order.step()
                dve.wait_ge(dve_order, order.value(k))
                dve.memset(ve[n][:], EPS).then_inc(dve_order, 1)
                order.step()
                for t in range(TT):
                    dve.bn_aggr(mv[n][:, t], st[n][:, t]).then_inc(dve_order, 1)
                    last = order.step()
                dve.wait_ge(dve_order, order.value(last))
                dve.tensor_tensor(ve[n][:], mv[n][:, :, 1], ve[n][:], ALU.add).then_inc(var_ready[n], 1)

            def normalise(n, count, src, dst):
                dve.wait_ge(rstd_ready[n], count)
                for t in range(TT):
                    ins = dve.tensor_scalar(dst[:, t], src[:, t], mv[n][:, t, 0:1], rstd[n][:, t:t + 1],
                                            ALU.subtract, ALU.mult)
                    ins.then_inc(dve_order, 1)
                    k = order.step()
                return k

            def embedding_stats(made):
                statistics("x", xf, sem["x_in"], 16 * (made + 1))

            def embedding(made):
                if reached(made):
                    dve.wait_ge(sem["emb_T"], DH * made)
                if reached(made):
                    dve.wait_ge(sem["embb_made"], made)
                k = normalise("x", made + 1, xf, emb)
                dve.wait_ge(sem["ctx_arrived"], 16 * (made + 1))
                dve.wait_ge(dve_order, order.value(k))
                dve.tensor_tensor(emb[:], emb[:], ctxf[:], ALU.add).then_inc(sem["emb_ready"], 1)

            def embedding_low(i):
                for h in range(DH):
                    dve.wait_ge(sem["embT_hi"], DH * i + h + 1)
                    dve.tensor_tensor(embTl[:, h], psum[6 + h], embTh[:, h].bitcast(F32),
                                      ALU.subtract).then_inc(sem["embT_lo"], 1)

            def embedding_bias(i):
                dve.wait_ge(sem["emb_ready"], i + 1)
                dve.tensor_tensor(embb[:], emb[:], row(0), ALU.add).then_inc(sem["embb_made"], 1)

            def k_maxima(i):
                for h in range(DH):
                    dve.wait_ge(sem["qkv_done"], QKV * i + h + 1)
                    dve.tensor_reduce(km[:, h:h + 1], psum[h], AX_X, ALU.max).then_inc(dve_order, 1)
                    k = order.step()
                dve.wait_ge(dve_order, order.value(k))
                dve.tensor_tensor(kmb[:], km[:], cols[:, 1], ALU.add).then_inc(dve_order, 1)
                k = order.step()
                dve.wait_ge(dve_order, order.value(k))
                dve.tensor_tensor(kb[:], cols[:, 1], kmb[:], ALU.subtract).then_inc(sem["kb_ready"], 1)

            def ek_times_v(i):
                for h in range(DH):
                    dve.wait_ge(sem["qkv_done"], QKV * i + DH + h + 1)
                    dve.wait_ge(sem["ek_ready"], DH * i + h + 1)
                    dve.scalar_tensor_tensor(ekvT[:, h], psum[2 + h], cols[:, 2, h:h + 1], ekT[:, h],
                                             ALU.add, ALU.mult).then_inc(sem["ekv_ready"], 1)

            def ek_low(i):
                for j in range(TT):
                    dve.wait_ge(sem["EK_hi"], TT * i + j + 1)
                    dve.tensor_tensor(EKl[:, j], psum[6 + j % 2], EKh[:, j].bitcast(F32),
                                      ALU.subtract).then_inc(sem["EK_lo"], 1)

            def gate(i):
                for h in range(DH):
                    bank_den, bank_num = SUMS_BANKS[h]
                    dve.wait_ge(sem["sums_done"], 2 * (DH * i + h) + 1)
                    dve.wait_ge(sem["eq_ready"], DH * i + h + 1)
                    dve.scalar_tensor_tensor(yT[:, h], eq[:, h], 1.0, psum[bank_den], ALU.add, ALU.mult).then_inc(sem["den_read"], 1)
                    dve.wait_ge(sem["den_read"], DH * i + h + 1)
                    dve.reciprocal(yT[:, h], yT[:, h]).then_inc(dve_order, 1)
                    k = order.step()
                    dve.wait_ge(sem["sums_done"], 2 * (DH * i + h) + 2)
                    dve.wait_ge(dve_order, order.value(k))
                    dve.tensor_tensor(yT[:, h], psum[bank_num], yT[:, h], ALU.mult).then_inc(sem["y_ready"], 1)

            def attention_sum(j):
                dve.wait_ge(sem["embb_made"], j + 1)
                for t in range(TT):
                    dve.wait_ge(sem["attn_done"], TT * j + t + 1)
                    dve.tensor_tensor(a_sb[:, t], psum[6 + t % 2][:, 0:D], embb[:, t], ALU.add).then_inc(sem["s_added"], 1)
                statistics("a", a_sb, sem["s_added"], TT * j + 1, 1)

            def attention_norm(j):
                k = normalise("a", j + 1, a_sb, a_sb)
                dve.wait_ge(dve_order, order.value(k))
                dve.tensor_tensor(a_sb[:], a_sb[:], row(1), ALU.mult).then_inc(dve_order, 1)
                k = order.step()
                dve.wait_ge(dve_order, order.value(k))
                dve.tensor_tensor(a_sb[:], a_sb[:], row(2), ALU.add).then_inc(sem["a_ready"], 1)
                dve.wait_ge(sem["a_ready"], j + 1)
                dve.wait_ge(sem["xb_in"], 16 * (j + 1))
                dve.tensor_tensor(ab2[:], a_sb[:], row(3), ALU.add).then_inc(dve_order, 1)
                return order.step()

            def a_low(j):
                for h in range(DH):
                    dve.wait_ge(sem["aT_hi"], DH * j + h + 1)
                    dve.tensor_tensor(aTl[:, h], psum[4 + h], aTh[:, h].bitcast(F32),
                                      ALU.subtract).then_inc(sem["aT_lo"], 1)

            def block_output(j, k_ab2):
                dve.wait_ge(dve_order, order.value(k_ab2))
                for t in range(TT):
                    dve.wait_ge(sem["ffn2_done"], TT * j + t + 1)
                    dve.tensor_tensor(ab2[:, t], psum[4 + t % 2][:, 0:D], ab2[:, t], ALU.add).then_inc(sem["s2_added"], 1)
                statistics("f", ab2, sem["s2_added"], TT * j + 1, 1)
                k = normalise("f", j + 1, ab2, ab2)
                dve.wait_ge(dve_order, order.value(k))
                dve.tensor_tensor(ab2[:], ab2[:], row(1), ALU.mult).then_inc(dve_order, 1)
                k = order.step()
                dve.wait_ge(dve_order, order.value(k))
                dve.tensor_tensor(ab2[:], ab2[:], row(2), ALU.add).then_inc(dve_order, 1)
                k = order.step()
                dve.wait_ge(sem["xb_in"], 16 * (j + 1))
                dve.wait_ge(dve_order, order.value(k))
                dve.tensor_tensor(ab2[:], ab2[:], xb[:], ALU.add).then_inc(sem["x1_ready"], 1)
                statistics("z", ab2, sem["x1_ready"], j + 1)
                dve.wait_ge(rstd_ready["z"], j + 1)
                for t in range(TT):
                    dve.tensor_scalar(z_sb[:, t], ab2[:, t], mv["z"][:, t, 0:1], rstd["z"][:, t:t + 1],
                                      ALU.subtract, ALU.mult).then_inc(sem["z_ready"], 1)
                dve.wait_ge(sem["z16_hi"], j + 1)
                dve.scalar_tensor_tensor(z16l[:, j], z_sb[:], Z_SCALE, z16h[:, j],
                                         ALU.mult, ALU.subtract).then_inc(sem["z16_lo"], 1)

            def z_low(j):
                for h in range(DH):
                    dve.wait_ge(sem["zT_hi"], DH * j + h + 1)
                    dve.tensor_tensor(zTl[:, h, j], psum[4 + h], zTh[:, h, j].bitcast(F32),
                                      ALU.subtract).then_inc(sem["zT_lo"], 1)

            order = Order(0)
            embedding_stats(0)
            embedding(0)
            dve.wait_ge(sem["vectors_in"], 16 * 8)
            dve.tensor_scalar(nbq[:], cols[:, 0], -1.0, None, ALU.mult).then_inc(sem["nbq_ready"], 1)
            embedding_low(0)
            embedding_bias(0)
            k_maxima(0)
            ek_times_v(0)
            dve.wait_ge(sem["band_masked"], 1)
            dve.tensor_reduce(wmax[:], pos[:], AX_X, ALU.max).then_inc(dve_order, 1)
            k = order.step()
            dve.wait_ge(dve_order, order.value(k))
            dve.tensor_scalar(nwmax[:], wmax[:], -1.0, None, ALU.mult).then_inc(sem["wmax_ready"], 1)
            for j in range(TT):
                dve.wait_ge(sem["ewT_hi"], j + 1)
                dve.tensor_tensor(ewTl[:, j], psum[4 + j % 2], ewTh[:, j].bitcast(F32), ALU.subtract).then_inc(sem["ewT_lo"], 1)
            ek_low(0)
            embedding_stats(1)
            embedding(1)
            gate(0)
            assert order.k == STEPS_A0, order.k
            with dve.Fori(1, B) as i:
                order = Order(STEPS_A0 + STEPS_A * (i - 1))
                attention_sum(i - 1)
                embedding_low(i)
                embedding_bias(i)
                k_ab2 = attention_norm(i - 1)
                k_maxima(i)
                ek_times_v(i)
                a_low(i - 1)
                ek_low(i)
                embedding_stats(i + 1)
                embedding(i + 1)
                block_output(i - 1, k_ab2)
                gate(i)
                z_low(i - 1)
                assert order.k == STEPS_A, order.k
            order = Order(STEPS_A0 + STEPS_A * (B - 1))
            attention_sum(B - 1)
            k_ab2 = attention_norm(B - 1)
            a_low(B - 1)
            block_output(B - 1, k_ab2)
            z_low(B - 1)
            assert order.k == STEPS_A1, order.k

            dve.wait_ge(sem["x1_spilled"], 16 * B)
            dve.wait_ge(sem["z16_lo"], B)
            dve.wait_ge(sem["zT_lo"], DH * B)
            dve.memset(acc[:], 0.0).then_inc(sem["zeroed"], 1)
            dve.memset(S[:], 0.0).then_inc(sem["zeroed"], 1)
            dve.memset(nR[:], -LOWEST).then_inc(sem["zeroed"], 1)
            dve.wait_ge(sem["zeroed"], 3)

            def phi_low(n):
                dve.wait_ge(sem["phi_hi"], n + 1)
                dve.tensor_tensor(phil[:, n % 2], phi_raw[:], phih[:, n % 2].bitcast(F32), ALU.subtract).then_inc(sem["phi_lo"], 1)

            def maxima(n, m):
                L = logits_ps[m % 2]
                dve.wait_ge(sem["l0_copied"], TT * n + m + 1)
                dve.tensor_reduce(cmax[:, m], L, AX_X, ALU.max).then_inc(dve_order, 1)
                k_c = order.step()
                dve.tensor_tensor(mx[:], L[:, 1], l0c[:], ALU.max).then_inc(dve_order, 1)
                k_m = order.step()
                dve.wait_ge(dve_order, order.value(k_c))
                dve.scalar_tensor_tensor(nRn[:, m], cmax[:, m], -1.0, nR[:, m], ALU.mult, ALU.min).then_inc(dve_order, 1)
                k_r = order.step()
                dve.wait_ge(dve_order, order.value(k_m))
                dve.tensor_tensor(mx[:], L[:, 2], mx[:], ALU.max).then_inc(dve_order, 1)
                k_m = order.step()
                dve.wait_ge(dve_order, order.value(k_r))
                dve.tensor_tensor(dR[:, m], nRn[:, m], nR[:, m], ALU.subtract).then_inc(sem["nmax_ready"], 1)
                dve.wait_ge(dve_order, order.value(k_m))
                dve.tensor_tensor(mx[:], L[:, 3], mx[:], ALU.max).then_inc(dve_order, 1)
                k_m = order.step()
                dve.wait_ge(sem["nmax_ready"], TT * n + m + 1)
                dve.tensor_copy(nR[:, m], nRn[:, m]).then_inc(dve_order, 1)
                order.step()
                return k_m

            def less_maximum(n, m, k_m):
                if reached(n) or m >= 2:
                    dve.wait_ge(sem["disp_lo"], TT * n + m - 1)
                dve.wait_ge(dve_order, order.value(k_m))
                dve.tensor_tensor(ed[:, m % 2], logits_ps[m % 2], mx[:].rearrange("p (a n) -> p a n", a=1).broadcast_to([P, B, CS]),
                                  ALU.subtract).then_inc(sem["sub_ready"], 1)

            def dispatch(n, m):
                e = ed[:, m % 2]
                dve.wait_ge(sem["e_ready"], TT * n + m + 1)
                dve.tensor_tensor(s01[:], e[:, 0:2], e[:, 2:4], ALU.add).then_inc(dve_order, 1)
                k = order.step()
                dve.wait_ge(dve_order, order.value(k))
                dve.tensor_tensor(ssum[:], s01[:, 0], s01[:, 1], ALU.add).then_inc(dve_order, 1)
                k = order.step()
                dve.wait_ge(dve_order, order.value(k))
                dve.reciprocal(ssum[:], ssum[:]).then_inc(dve_order, 1)
                k = order.step()
                dve.wait_ge(dve_order, order.value(k))
                dve.scalar_tensor_tensor(e, e, D_SCALE, ssum[:].rearrange("p (a n) -> p a n", a=1).broadcast_to([P, B, CS]),
                                         ALU.mult, ALU.mult).then_inc(sem["d_ready"], 1)

            def dispatch_low(n, m):
                dve.wait_ge(sem["disp_hi"], TT * n + m + 1)
                dve.tensor_tensor(displ[:, n % 2, m], ed[:, m % 2], disph[:, n % 2, m], ALU.subtract).then_inc(sem["disp_lo"], 1)

            def tile(n, m):
                k_m = maxima(n, m)
                if m >= 2:
                    dispatch_low(n, m - 2)
                less_maximum(n, m, k_m)
                if m >= 1:
                    dispatch(n, m - 1)

            def keep_alpha(c):
                dve.wait_ge(sem["alpha_ready"], TT * (c + 1))
                if reached(c):
                    dve.wait_ge(sem["acc_added"], 2 * TT * c)
                dve.tensor_copy(alpha_use[:], alpha[:]).then_inc(sem["alpha_kept"], 1)

            def add_bias(c):
                dve.wait_ge(sem["eb_in"], 16 * (c + 1))
                if reached(c):
                    dve.wait_ge(sem["y_moved"], 16 * CE * B * c)
                for j in range(CE // 2):
                    dve.wait_ge(sem["y_done"], (CE // 2) * c + j + 1)
                    bank = psum[6 + j % 2].rearrange("p (n e) -> p n e", n=2)
                    dve.tensor_tensor(y_sb[:, 2 * j:2 * j + 2], bank, ebb[:, 2 * j:2 * j + 2],
                                      ALU.add).then_inc(sem["y_ready_b"], 1)

            def accumulate(c, m):
                for k in range(2):
                    dve.wait_ge(sem["out_done"], 2 * (TT * c + m) + k + 1)
                    for q in range(2):
                        b = 2 * k + q
                        ins = dve.scalar_tensor_tensor(acc[:, b, m], acc[:, b, m], alpha_use[:, m, b:b + 1],
                                                       psum[4 + k][:, q * D:(q + 1) * D], ALU.mult, ALU.add)
                    ins.then_inc(sem["acc_added"], 1)

            BASE_B = STEPS_A0 + STEPS_A * (B - 1) + STEPS_A1
            order = Order(BASE_B)
            phi_low(0)
            for m in range(TT):
                tile(0, m)
            dispatch_low(0, TT - 2)
            dispatch(0, TT - 1)
            dispatch_low(0, TT - 1)
            assert order.k == STEPS_B, order.k

            def step(c, n=None):
                keep_alpha(c)
                dve.wait_ge(sem["alpha_kept"], c + 1)
                if n is not None:
                    phi_low(n)
                    tile(n, 0)
                    tile(n, 1)
                add_bias(c)
                if n is not None:
                    tile(n, 2)
                    tile(n, 3)
                    accumulate(c, 0)
                    dispatch_low(n, TT - 2)
                    dispatch(n, TT - 1)
                    accumulate(c, 1)
                    dispatch_low(n, TT - 1)
                    accumulate(c, 2)
                    accumulate(c, 3)
                else:
                    for m in range(TT):
                        accumulate(c, m)

            order = Order(BASE_B + STEPS_B)
            step(0, 1)
            assert order.k == STEPS_B, order.k
            with dve.Fori(1, CH - 1) as c:
                order = Order(BASE_B + STEPS_B * (c + 1))
                step(c, c + 1)
                assert order.k == STEPS_B, order.k
            step(CH - 1)
            dve.wait_ge(sem["s_ready"], TT * CH)
            dve.reciprocal(rS[:], S[:]).then_inc(sem["rS_ready"], 1)
            dve.wait_ge(sem["rS_ready"], 1)
            dve.wait_ge(sem["acc_added"], 2 * TT * CH)
            dve.wait_ge(sem["x1_back"], 16 * B)
            for b in range(B):
                for m in range(TT):
                    dve.scalar_tensor_tensor(acc[:, b, m], acc[:, b, m], rS[:, m, b:b + 1], x1_view[:, b, m],
                                             ALU.mult, ALU.add).then_inc(sem["out_ready"], 1)

        @block.tensor
        def _(pe):
            def split3(out_ap, Lh, Ll, Rh, Rl, start, stop):
                pe.matmul(out_ap, Lh, Rh, start=start, stop=False)
                pe.matmul(out_ap, Lh, Rl, start=False, stop=False)
                return pe.matmul(out_ap, Ll, Rh, start=False, stop=stop)

            def transposes(bank, sources):
                for q, src in enumerate(sources):
                    mm = pe.transpose(bank[:, q * P:(q + 1) * P], src, ident[:])
                return mm

            def t_emb(i):
                pe.wait_ge(sem["emb_ready"], i + 1)
                for h in range(DH):
                    if reached(i):
                        pe.wait_ge(sem["s_added"], TT * (i - 1) + 2 + h + 1)
                    transposes(psum[6 + h], [emb[:, t, h * P:(h + 1) * P] for t in range(TT)]).then_inc(sem["emb_T"], 1)

            def qkv(i):
                pe.wait_ge(sem["embT_lo"], DH * (i + 1))
                for turn, w in enumerate((1, 2, 0)):
                    for e in range(DH):
                        bank = psum[(0, 2, 0)[turn] + e]
                        if turn == 2:
                            pe.wait_ge(sem["ek_ready"], DH * i + e + 1)
                        elif reached(i) and e == 0:
                            pe.wait_ge(sem["den_read"], DH * (i - 1) + (2, 1)[turn])
                        elif reached(i):
                            pe.wait_ge(sem["y_ready"], DH * (i - 1) + (2, 1)[turn])
                        for h in range(DH):
                            mm = split3(bank, wqkvh[:, w, h, e * P:(e + 1) * P], wqkvl[:, w, h, e * P:(e + 1) * P],
                                        embTh[:, h], embTl[:, h], h == 0, h == DH - 1)
                        mm.then_inc(sem["qkv_done"], 1)

            def t_ek(i):
                pe.wait_ge(sem["ekv_ready"], DH * (i + 1))
                for j in range(TT):
                    if j < 2:
                        pe.wait_ge(sem["embT_lo"], DH * i + j + 1)
                    else:
                        pe.wait_ge(sem["EK_lo"], TT * i + j - 1)
                    transposes(psum[6 + j % 2], [src[:, h, j * P:(j + 1) * P] for src in (ekT, ekvT)
                                                 for h in range(DH)]).then_inc(sem["ek_T"], 1)

            def aft(i):
                pe.wait_ge(sem["EK_lo"], TT * (i + 1))
                for h in range(DH):
                    for kind in range(2):
                        bank = psum[SUMS_BANKS[h][kind]]
                        if h == 0:
                            pe.wait_ge(sem["ekv_ready"], DH * i + kind + 1)
                        else:
                            pe.wait_ge(sem["eq_ready"], DH * i + kind + 1)
                        c0 = kind * D + h * P
                        for j in range(TT):
                            mm = split3(bank, EKh[:, j, c0:c0 + P], EKl[:, j, c0:c0 + P], ewTh[:, j], ewTl[:, j],
                                        j == 0, j == TT - 1)
                        mm.then_inc(sem["sums_done"], 1)

            def attention(j):
                pe.wait_ge(sem["y_ready"], DH * (j + 1))
                for t in range(TT):
                    bank = psum[6 + t % 2]
                    if t < 2:
                        pe.wait_ge(sem["EK_lo"], TT * j + t + 3)
                    else:
                        pe.wait_ge(sem["s_added"], TT * j + t - 1)
                    for h in range(DH):
                        mm = pe.matmul(bank[:, 0:D], yT[:, h, t * P:(t + 1) * P], wo_sb[:, h],
                                       start=(h == 0), stop=(h == DH - 1))
                    mm.then_inc(sem["attn_done"], 1)

            def t_a(j):
                pe.wait_ge(sem["a_ready"], j + 1)
                for h in range(DH):
                    transposes(psum[4 + h], [a_sb[:, t, h * P:(h + 1) * P] for t in range(TT)]).then_inc(sem["a_T"], 1)

            def ffn(j):
                pe.wait_ge(sem["aT_lo"], DH * (j + 1))
                for m in range(HT):
                    bank = psum[4 + m % 2]
                    if m >= 2:
                        pe.wait_ge(sem["h_ready"], HT * j + m - 1)
                    for h in range(DH):
                        mm = split3(bank, w1h[:, h, m * P:(m + 1) * P], w1l[:, h, m * P:(m + 1) * P],
                                    aTh[:, h], aTl[:, h], h == 0, h == DH - 1)
                    mm.then_inc(sem["ffn1_done"], 1)
                for t in range(TT):
                    bank = psum[4 + t % 2]
                    if t >= 2:
                        pe.wait_ge(sem["s2_added"], TT * j + t - 1)
                    else:
                        pe.wait_ge(sem["h_ready"], HT * j + HT - 1 + t)
                    for m in range(HT):
                        if t == 0:
                            pe.wait_ge(sem["h_ready"], HT * j + m + 1)
                        mm = pe.matmul(bank[:, 0:D], hT[:, m, t * P:(t + 1) * P], w2_sb[:, m],
                                       start=(m == 0), stop=(m == HT - 1))
                    mm.then_inc(sem["ffn2_done"], 1)

            def t_z(j):
                pe.wait_ge(sem["z_ready"], TT * (j + 1))
                for h in range(DH):
                    pe.wait_ge(sem["s2_added"], TT * j + 2 + h + 1)
                    transposes(psum[4 + h], [z_sb[:, t, h * P:(h + 1) * P] for t in range(TT)]).then_inc(sem["z_T"], 1)

            pe.wait_ge(sem["ident_made"], 1)
            t_emb(0)
            pe.wait_ge(sem["wqkv_lo"], 1)
            qkv(0)
            pe.wait_ge(sem["ew_ready"], TT)
            for j in range(TT):
                if j >= 2:
                    pe.wait_ge(sem["ewT_lo"], j - 1)
                for t in range(TT):
                    mm = pe.transpose(psum[4 + j % 2][:, t * P:(t + 1) * P], pos[:, t, j * P:(j + 1) * P], ident[:])
                mm.then_inc(sem["ew_T"], 1)
            t_ek(0)
            pe.wait_ge(sem["ewT_lo"], TT)
            aft(0)
            pe.wait_ge(sem["wo_w2_in"], 32)
            pe.wait_ge(sem["w1_lo"], 1)
            with pe.Fori(1, B) as i:
                attention(i - 1)
                t_emb(i)
                qkv(i)
                t_a(i - 1)
                t_ek(i)
                ffn(i - 1)
                aft(i)
                t_z(i - 1)
            attention(B - 1)
            t_a(B - 1)
            ffn(B - 1)
            t_z(B - 1)

            def logits(n, m):
                if m == 0:
                    pe.wait_ge(sem["phi_lo"], n + 1)
                if reached(n) or m >= 2:
                    pe.wait_ge(sem["e2_ready"], TT * n + m - 1)
                for b in range(B):
                    for h in range(DH):
                        mm = split3(logits_ps[m % 2][:, b], zTh[:, h, b, m * P:(m + 1) * P], zTl[:, h, b, m * P:(m + 1) * P],
                                    phih[:, n % 2, h], phil[:, n % 2, h], h == 0, h == DH - 1)
                mm.then_inc(sem["l_full"], 1)

            def t_combine(n, m):
                pe.wait_ge(sem["e2_ready"], TT * n + m + 1)
                for k in range(SUB):
                    if m >= 1:
                        pe.wait_ge(sem["combT_ready"], SUB * (TT * n + m - 1) + k + 1)
                    elif reached(n):
                        pe.wait_ge(sem["y_ready_b"], (CE // 2) * (n - 1) + 2 + k + 1)
                    transposes(psum[6 + k], [e2[:, m, b, k * P:(k + 1) * P] for b in range(B)]).then_inc(sem["comb_T"], 1)

            def slots(c, b):
                if b == 0:
                    pe.wait_ge(sem["disp_lo"], TT * (c + 1))
                bank = psum[4 + b % 2]
                if b >= 2:
                    pe.wait_ge(sem["slotsT_ready"], B * c + b - 1)
                elif reached(c):
                    pe.wait_ge(sem["acc_added"], 2 * TT * (c - 1) + 2 * TT - 1 + b)
                for h in range(DH):
                    for m in range(TT):
                        hs = slice(h * P, (h + 1) * P)
                        mm = split3(bank[:, h * CS:(h + 1) * CS], z16h[:, b, m, hs], z16l[:, b, m, hs],
                                    disph[:, c % 2, m, b], displ[:, c % 2, m, b], m == 0, m == TT - 1)
                mm.then_inc(sem["slots_done"], 1)

            def experts(c):
                pe.wait_ge(sem["slotsT_ready"], B * (c + 1))
                for j in range(CE // 2):
                    bank = psum[6 + j % 2]
                    if j >= 2:
                        pe.wait_ge(sem["y_ready_b"], (CE // 2) * c + j - 1)
                    else:
                        pe.wait_ge(sem["combT_ready"], SUB * TT * (c + 1) - 1 + j)
                    if j % 2 == 0:
                        pe.wait_ge(W_in[j // 2], 16 * (c + 1))
                    for q in range(2):
                        for h in range(DH):
                            mm = pe.matmul(bank[:, q * D:(q + 1) * D],
                                           slotsT[:, h, 2 * j + q].rearrange("p b s -> p (b s)"), Wr[:, 2 * j + q, h],
                                           start=(h == 0), stop=(h == DH - 1))
                    mm.then_inc(sem["y_done"], 1)

            def combine(c, m):
                if m == 0:
                    pe.wait_ge(sem["y_moved"], 16 * CE * B * (c + 1))
                    pe.wait_ge(sem["combT_ready"], SUB * TT * (c + 1))
                for k in range(2):
                    bank = psum[4 + k]
                    if m >= 1:
                        pe.wait_ge(sem["acc_added"], 2 * (TT * c + m - 1) + k + 1)
                    else:
                        pe.wait_ge(sem["slotsT_ready"], B * c + 2 + k + 1)
                    for q in range(2):
                        b = 2 * k + q
                        for u in range(SUB):
                            mm = pe.matmul(bank[:, q * D:(q + 1) * D], combT[:, u, b, m], y_c[:, u, b],
                                           start=(u == 0), stop=(u == SUB - 1))
                    mm.then_inc(sem["out_done"], 1)

            pe.wait_ge(sem["zT_lo"], DH * B)
            for m in range(TT):
                logits(0, m)
                if m >= 1:
                    t_combine(0, m - 1)
            t_combine(0, TT - 1)

            def step(c, n=None):
                slots(c, 0)
                if n is not None:
                    logits(n, 0)
                slots(c, 1)
                slots(c, 2)
                if n is not None:
                    logits(n, 1)
                slots(c, 3)
                if n is not None:
                    logits(n, 2)
                experts(c)
                if n is not None:
                    logits(n, 3)
                for m in range(TT):
                    combine(c, m)
                    if n is not None:
                        t_combine(n, m)

            step(0, 1)
            with pe.Fori(1, CH - 1) as c:
                step(c, c + 1)
            step(CH - 1)


_INS = ["x", "ctx_1024", "L0_xattn_wq", "L0_xattn_bq", "L0_xattn_wk", "L0_xattn_bk", "L0_xattn_wv", "L0_xattn_bv",
        "L0_xattn_wo", "L0_xattn_bo", "L0_xattn_pos_bias", "L0_xattn_gamma", "L0_xattn_beta", "L0_xattn_w1",
        "L0_xattn_b1", "L0_xattn_w2", "L0_xattn_b2", "L0_ffn_phi", "L0_ffn_W", "L0_ffn_b"]
_OUTS = [((4, 512, 256), "float32")]


def kernel(**inputs):
    import numpy as _np
    import concourse.bacc as _bacc
    from concourse import mybir as _mybir
    from concourse.bass_utils import run_bass_kernel_spmd as _run

    nc = _bacc.Bacc("TRN2", target_bir_lowering=False, num_devices=1)
    arrays, args = {}, []
    for name in _INS:
        a = _np.ascontiguousarray(inputs[name])
        arrays[f"in_{name}_dram"] = a
        args.append(nc.dram_tensor(f"in_{name}_dram", a.shape, _mybir.dt.from_np(a.dtype), kind="ExternalInput").ap())
    for i, (shape, dtype) in enumerate(_OUTS):
        dt = _mybir.dt.from_np(_np.dtype(dtype))
        args.append(nc.dram_tensor(f"out_{i}_dram", shape, dt, kind="ExternalOutput").ap())
    bass_aft_soft_moe(nc, *args)
    r = _run(nc, [arrays], core_ids=[0])
    return r.results[0]["out_0_dram"]
```

```python
from contextlib import ExitStack

import concourse.bass as bass
from concourse import mybir

F32 = mybir.dt.float32
F32R = mybir.dt.float32r
F16 = mybir.dt.float16
ALU = mybir.AluOpType
ACT = mybir.ActivationFunctionType
AX_X = mybir.AxisListType.X


def reached(n, first=1):
    return not isinstance(n, int) or n >= first


class Order:

    def __init__(self, base):
        self.base, self.k = base, 0

    def step(self):
        self.k += 1
        return self.k

    def value(self, k):
        return self.base + k


def bass_aft_soft_moe(nc, x, ctx_in, wq, bq, wk, bk, wv, bv, wo, bo, pos_bias, gamma, beta,
                      w1, b1, w2, b2, phi, W, eb, out):
    P = 128
    B, T, D = x.shape
    H = w1.shape[1]
    NE, _, PE_ = phi.shape[1], phi.shape[0], phi.shape[2]
    NS = NE * PE_
    TT = T // P
    DH = D // P
    HT = H // P
    CE = 8
    CS = CE * PE_
    CH = NE // CE
    SUB = CS // P
    EPS = 1e-5
    BAND = 64
    Z_SCALE = 256.0
    D_SCALE = 4096.0
    LOWEST = -3.0e38
    QKV = 3 * DH
    OUT_BANKS = (4, 6, 4, 6)
    COMB_BANKS = (4, 6, 6, 6)
    SUMS_BANKS = ((2, 3), (0, 1))
    STEPS_A0, STEPS_A1, STEPS_A, STEPS_A2, STEPS_B0, STEPS_B = 32, 33, 57, 63, 28, 24
    assert B * PE_ == P and SUB == 2 and DH == 2 and TT == 4

    x_d = x.rearrange("b (t p) d -> b p t d", p=P)
    ctx_d = ctx_in.rearrange("b (t p) d -> b p t d", p=P)
    out_d = out.rearrange("b (t p) d -> b p t d", p=P)
    phi_d = phi.rearrange("(h p) (c n) s -> c p h (n s)", p=P, n=CE)
    eb_d = eb.rearrange("(c n) e -> c (n e)", n=CE)
    W_d = W.rearrange("(c n) (h p) e -> c p n h e", p=P, n=CE)
    spill = nc.dram_tensor("x1_spill", (B, T, D), F32, kind="Internal").ap()
    spill_d = spill.rearrange("b (t p) d -> b p t d", p=P)

    with ExitStack() as stack:
        def sb(name, shape, dt, where=stack):
            return where.enter_context(nc.sbuf_tensor(name, shape, dt))

        logits_ps = [stack.enter_context(nc.psum_tensor(f"ps_pair{i}", [P, B, CS], F32))[:, :, :] for i in range(2)]
        psum = [logits_ps[k // 2][:, 2 * (k % 2):2 * (k % 2) + 2, :].rearrange("p a n -> p (a n)") for k in range(4)]
        psum += [stack.enter_context(nc.psum_tensor(f"ps{k}", [P, 512], F32))[:, :] for k in range(4, 8)]

        ident = sb("ident", [P, P], F32)
        zTh = sb("zTh", [P, DH, B, T], F32R)
        zTl = sb("zTl", [P, DH, B, T], F32R)
        z16h = sb("z16h", [P, B, TT, D], F16)
        z16l = sb("z16l", [P, B, TT, D], F16)

        stage_a = ExitStack()
        ewTh = sb("ewTh", [P, TT, T], F32R, stage_a)
        ewTl = sb("ewTl", [P, TT, T], F32R, stage_a)
        EKh = sb("EKh", [P, TT, 2 * D], F32R, stage_a)
        EKl = sb("EKl", [P, TT, 2 * D], F32R, stage_a)
        wqkvh = sb("wqkvh", [P, 3, DH, D], F32R, stage_a)
        wqkvl = sb("wqkvl", [P, 3, DH, D], F32R, stage_a)
        setup = ExitStack()
        pos = sb("pos", [P, TT, T], F32, setup)
        wqkv_raw = sb("wqkv_raw", [P, 3, DH, D], F32, setup)
        w1_raw = sb("w1_raw", [P, DH, H], F32, setup)
        setup.close()
        hT = sb("hT", [P, HT, T], F32, stage_a)
        aTh = sb("aTh", [P, DH, T], F32R, stage_a)
        aTl = sb("aTl", [P, DH, T], F32R, stage_a)
        xf = sb("xf", [P, TT, D], F32, stage_a)
        ctxf = sb("ctxf", [P, TT, D], F32, stage_a)
        emb = sb("emb", [P, TT, D], F32, stage_a)
        embb = sb("embb", [P, TT, D], F32, stage_a)
        embTh = sb("embTh", [P, DH, T], F32R, stage_a)
        embTl = sb("embTl", [P, DH, T], F32R, stage_a)
        wo_sb = sb("wo_sb", [P, DH, D], F32, stage_a)
        w1h = sb("w1h", [P, DH, H], F32R, stage_a)
        w1l = sb("w1l", [P, DH, H], F32R, stage_a)
        w2_sb = sb("w2_sb", [P, HT, D], F32, stage_a)
        rows = sb("rows", [P, 4, D], F32, stage_a)
        cols = sb("cols", [P, 3, DH], F32, stage_a)
        nbq = sb("nbq", [P, DH], F32, stage_a)
        b1c = sb("b1c", [P, HT], F32, stage_a)
        km = sb("km", [P, DH], F32, stage_a)
        kmb = sb("kmb", [P, DH], F32, stage_a)
        kb = sb("kb", [P, DH], F32, stage_a)
        wmax = sb("wmax", [P, TT], F32, stage_a)
        nwmax = sb("nwmax", [P, TT], F32, stage_a)
        mhalf = sb("mhalf", [P, TT], F32, stage_a)
        LN = ("x", "a", "f", "z")
        st = {n: sb(f"st_{n}", [P, TT, 6], F32, stage_a) for n in LN}
        mv = {n: sb(f"mv_{n}", [P, TT, 2], F32, stage_a) for n in LN}
        ve = {n: sb(f"ve_{n}", [P, TT], F32, stage_a) for n in LN}
        rstd = {n: sb(f"rstd_{n}", [P, TT], F32, stage_a) for n in LN}
        a_sb = sb("a_sb", [P, TT, D], F32, stage_a)
        ab2 = sb("ab2", [P, TT, D], F32, stage_a)
        xb = sb("xb", [P, TT, D], F32, stage_a)
        z_sb = sb("z_sb", [P, TT, D], F32, stage_a)
        eq = sb("eq", [P, DH, T], F32, stage_a)
        ekT = sb("ekT", [P, DH, T], F32, stage_a)
        ekvT = sb("ekvT", [P, DH, T], F32, stage_a)
        yT = sb("yT", [P, DH, T], F32, stage_a)
        stage_a.close()

        Wr = sb("Wr", [P, CE, DH, D], F32)
        phi_raw = sb("phi_raw", [P, DH, CS], F32)
        phih = sb("phih", [P, 2, DH, CS], F32R)
        phil = sb("phil", [P, 2, DH, CS], F32R)
        ebb = sb("ebb", [P, CE, D], F32)
        slotsT = sb("slotsT", [P, DH, CE, B, PE_], F32)
        acc = sb("acc", [P, B, TT, D], F32)
        disph = sb("disph", [P, 2, TT, B, CS], F16)
        displ = sb("displ", [P, 2, TT, B, CS], F16)
        e2 = sb("e2", [P, TT, B, CS], F32)
        combT = sb("combT", [P, SUB, B, TT, P], F32)
        y_sb = sb("y_sb", [P, CE, D], F32)
        y_c = sb("y_c", [P, SUB, B, D], F32)
        mx = sb("mx", [P, CS], F32)
        ed = sb("ed", [P, 2, B, CS], F32)
        ssum = sb("ssum", [P, CS], F32)
        cmax = sb("cmax", [P, TT, B], F32)
        nR = sb("nR", [P, TT, B], F32)
        nRn = sb("nRn", [P, TT, B], F32)
        dR = sb("dR", [P, TT, B], F32)
        alpha = sb("alpha", [P, 2, TT, B], F32)
        csum = sb("csum", [P, TT, B], F32)
        S = sb("S", [P, TT, B], F32)
        rS = sb("rS", [P, TT, B], F32)

        def phi_by_slot(h):
            return phi_raw[:, h].rearrange("p (g e s) -> p g e s", g=SUB, s=PE_)

        x1_view = Wr[:].rearrange("p (b t) h e -> p b (t h) e", b=B)

        names = """ident_made consts_made band_masked x_in ctx_arrived xb_in wqkv_in w1_in pos_in vectors_in
            wo_w2_in pool_order dve_order wqkv_hi w1_hi wqkv_lo w1_lo wmax_ready ew_ready ew_T ewT_hi ewT_lo
            nbq_ready emb_ready embb_made emb_T embT_hi embT_lo qkv_done kb_ready ek_ready eq_ready
            ekv_ready ek_T EK_hi EK_lo sums_done den_read y_ready attn_done s_added a_ready a_T aT_hi aT_lo
            ffn1_done h_ready ffn2_done s2_added x1_ready x1_spilled z_ready z_T z16_hi z16_lo zT_hi zT_lo
            phi_in phi_hi phi_lo eb_in l_full nmax_ready sub_ready e_ready d_ready disp_hi disp_lo
            e2_ready alpha_ready slots_done slotsT_ready y_done y_ready_b comb_T combT_ready
            out_done acc_added s_ready rS_ready x1_back out_ready out_stored zeroed
            acc_zeroed""".split()
        sem = {n: stack.enter_context(nc.semaphore(n)) for n in names}
        dve_order = sem["dve_order"]
        var_ready = {n: stack.enter_context(nc.semaphore(f"var_ready_{n}")) for n in LN}
        rstd_ready = {n: stack.enter_context(nc.semaphore(f"rstd_ready_{n}")) for n in LN}
        y_moved = [stack.enter_context(nc.semaphore(f"y_moved{k}")) for k in range(2)]
        W_in = [stack.enter_context(nc.semaphore(f"W_in{g}")) for g in range(2)]

        block = stack.enter_context(nc.Block())

        @block.sync
        def _(sp):
            sp.dma_start(xf[:], x_d[0]).then_inc(sem["x_in"], 16)
            sp.dma_start(ctxf[:], ctx_d[0]).then_inc(sem["ctx_arrived"], 16)
            for i, w in enumerate((wq, wk, wv)):
                sp.dma_start(wqkv_raw[:, i], w.rearrange("(h p) e -> p h e", p=P)).then_inc(sem["wqkv_in"], 16)
            for i, v in enumerate((bo, gamma, beta, b2)):
                sp.dma_start(rows[:, i, :], v.rearrange("(a d) -> a d", a=1).broadcast_to([P, D])).then_inc(sem["vectors_in"], 16)
            for i, v in enumerate((bq, bk, bv)):
                sp.dma_start(cols[:, i, :], v.rearrange("(h p) -> p h", p=P), allow_slow_non_contiguous=True).then_inc(sem["vectors_in"], 16)
            sp.dma_start(b1c[:], b1.rearrange("(h p) -> p h", p=P), allow_slow_non_contiguous=True).then_inc(sem["vectors_in"], 16)
            sp.dma_start(pos[:], pos_bias.rearrange("(t p) j -> p t j", p=P)).then_inc(sem["pos_in"], 16)
            sp.dma_start(w1_raw[:], w1.rearrange("(h p) e -> p h e", p=P)).then_inc(sem["w1_in"], 16)
            sp.dma_start(wo_sb[:], wo.rearrange("(h p) e -> p h e", p=P)).then_inc(sem["wo_w2_in"], 16)
            sp.dma_start(w2_sb[:], w2.rearrange("(h p) e -> p h e", p=P)).then_inc(sem["wo_w2_in"], 16)

            def batch(d, b):
                return d[b] if isinstance(b, int) else d[bass.ds(b, 1)].rearrange("a p t d -> (a p) t d")

            def load_front(b, made):
                sp.wait_ge(sem["emb_ready"], made)
                sp.dma_start(xf[:], batch(x_d, b)).then_inc(sem["x_in"], 16)
                sp.dma_start(ctxf[:], batch(ctx_d, b)).then_inc(sem["ctx_arrived"], 16)

            def load_back(j):
                if reached(j):
                    sp.wait_ge(sem["x1_ready"], j)
                sp.dma_start(xb[:], batch(x_d, j)).then_inc(sem["xb_in"], 16)

            def store_back(j):
                sp.wait_ge(sem["x1_ready"], j + 1)
                sp.dma_start(batch(spill_d, j), ab2[:]).then_inc(sem["x1_spilled"], 16)

            load_front(1, 1)
            load_back(0)
            load_front(2, 2)
            with sp.Fori(2, B) as i:
                load_front((i + 1) % B, i + 1)
                store_back(i - 2)
                sp.wait_ge(sem["x1_spilled"], 16 * (i - 1))
                load_back(i - 1)
            store_back(B - 2)
            sp.wait_ge(sem["x1_spilled"], 16 * (B - 1))
            load_back(B - 1)

            def load_phi(c):
                if reached(c):
                    sp.wait_ge(sem["phi_lo"], c)
                src = phi_d[c] if isinstance(c, int) else phi_d[bass.ds(c, 1)].rearrange("a p h s -> (a p) h s")
                sp.dma_start(phi_raw[:], src).then_inc(sem["phi_in"], 16)

            def load_experts(c):
                src = W_d[c] if isinstance(c, int) else W_d[bass.ds(c, 1)].rearrange("a p n h e -> (a p) n h e")
                for g in range(2):
                    if reached(c):
                        sp.wait_ge(sem["y_done"], (CE // 2) * (c - 1) + 2 * g + 2)
                    sp.dma_start(Wr[:, 4 * g:4 * g + 4], src[:, 4 * g:4 * g + 4]).then_inc(W_in[g], 16)
                bias = eb_d[c:c + 1] if isinstance(c, int) else eb_d[bass.ds(c, 1)]
                if reached(c):
                    sp.wait_ge(sem["out_done"], 2 * TT * c)
                sp.dma_start(ebb[:].rearrange("p n e -> p (n e)"), bias.broadcast_to([P, CE * D])).then_inc(sem["eb_in"], 16)

            def move_y(c):
                for g in range(SUB):
                    sp.wait_ge(sem["y_ready_b"], (CE // 2) * c + 2 * g + 2)
                    for b in range(B):
                        sp.dma_start(y_c[:, g, b, :], y_sb[PE_ * b:PE_ * (b + 1), 4 * g:4 * g + 4, :]).then_inc(y_moved[b // 2], 16)

            sp.wait_ge(sem["sums_done"], 2 * DH * B)
            load_phi(0)
            load_experts(0)
            load_phi(1)
            store_back(B - 1)
            load_phi(2)
            move_y(0)
            with sp.Fori(1, CH - 2) as c:
                load_phi(c + 2)
                load_experts(c)
                move_y(c)
            for c in (CH - 2, CH - 1):
                load_experts(c)
                move_y(c)
            sp.wait_ge(sem["y_done"], (CE // 2) * CH)
            for b in range(B):
                sp.dma_start(x1_view[:, b], spill_d[b]).then_inc(sem["x1_back"], 16)
            for b in range(B):
                sp.wait_ge(sem["out_ready"], TT * (b + 1))
                sp.dma_start(out_d[b], acc[:, b]).then_inc(sem["out_stored"], 16)
            sp.wait_ge(sem["out_stored"], 16 * B)

        @block.gpsimd
        def _(pool):
            pool.memset(ident[:], 0.0).then_inc(sem["pool_order"], 1)
            pool.wait_ge(sem["pool_order"], 1)
            pool.affine_select(out=ident[:], in_=ident[:], compare_op=ALU.not_equal, fill=1.0, base=0,
                               pattern=[[-1, P]], channel_multiplier=1).then_inc(sem["ident_made"], 1)
            pool.memset(mhalf[:], -0.5).then_inc(sem["consts_made"], 1)
            pool.wait_ge(sem["consts_made"], 1)

            def inverse_deviation(n, count):
                pool.wait_ge(var_ready[n], count)
                pool.tensor_tensor(rstd[n][:], ve[n][:], mhalf[:], ALU.pow).then_inc(rstd_ready[n], 1)

            inverse_deviation("x", 1)
            pool.wait_ge(sem["wqkv_hi"], 1)
            pool.tensor_tensor(wqkvl[:], wqkv_raw[:], wqkvh[:].bitcast(F32), ALU.subtract).then_inc(sem["wqkv_lo"], 1)
            pool.wait_ge(sem["pos_in"], 16)
            pool.affine_select(out=pos[:], in_=pos[:], compare_op=ALU.is_ge, fill=0.0, base=BAND - 1,
                               pattern=[[P, TT], [-1, T]], channel_multiplier=1).then_inc(sem["pool_order"], 1)
            pool.wait_ge(sem["pool_order"], 2)
            pool.affine_select(out=pos[:], in_=pos[:], compare_op=ALU.is_ge, fill=0.0, base=BAND - 1,
                               pattern=[[-P, TT], [1, T]], channel_multiplier=-1).then_inc(sem["band_masked"], 1)
            pool.wait_ge(sem["w1_hi"], 1)
            pool.tensor_tensor(w1l[:], w1_raw[:], w1h[:].bitcast(F32), ALU.subtract).then_inc(sem["w1_lo"], 1)

            inverse_deviation("x", 2)
            inverse_deviation("a", 1)
            inverse_deviation("x", 3)
            with pool.Fori(2, B) as i:
                inverse_deviation("a", i)
                inverse_deviation("x", i + 2)
                inverse_deviation("f", i - 1)
                inverse_deviation("z", i - 1)
            inverse_deviation("a", B)
            for j in (B - 1, B):
                inverse_deviation("f", j)
                inverse_deviation("z", j)

            def rescale_sums(c):
                for m in range(TT):
                    pool.wait_ge(sem["alpha_ready"], TT * c + m + 1)
                    pool.tensor_tensor(S[:, m], S[:, m], alpha[:, c % 2, m], ALU.mult).then_inc(sem["pool_order"], 1)
                    pool.wait_ge(sem["pool_order"], TT * c + m + 3)
                    pool.tensor_tensor(S[:, m], S[:, m], csum[:, m], ALU.add).then_inc(sem["s_ready"], 1)
                    pool.wait_ge(sem["disp_hi"], TT * c + m + 1)
                    pool.tensor_tensor(displ[:, c % 2, m], ed[:, m % 2], disph[:, c % 2, m], ALU.subtract).then_inc(sem["disp_lo"], 1)

            pool.wait_ge(sem["ffn2_done"], TT * B)
            pool.memset(acc[:], 0.0).then_inc(sem["acc_zeroed"], 1)
            pool.wait_ge(sem["zeroed"], 2)
            rescale_sums(0)
            with pool.Fori(1, CH) as c:
                pool.wait_ge(sem["s_ready"], TT * c)
                rescale_sums(c)

        @block.scalar
        def _(act):
            def embedding_high(i):
                for h in range(DH):
                    act.wait_ge(sem["emb_T"], DH * i + h + 1)
                    act.activation(embTh[:, h], psum[6 + h], ACT.Copy).then_inc(sem["embT_hi"], 1)

            def exp_kq(i):
                for h in range(DH):
                    act.wait_ge(sem["qkv_done"], QKV * i + h + 1)
                    act.wait_ge(sem["kb_ready"], i + 1)
                    act.activation(ekT[:, h], psum[h], ACT.Exp, bias=kb[:, h:h + 1]).then_inc(sem["ek_ready"], 1)
                for h in range(DH):
                    act.wait_ge(sem["qkv_done"], QKV * i + 2 * DH + h + 1)
                    if reached(i):
                        act.wait_ge(sem["den_read"], DH * i)
                    act.activation(eq[:, h], psum[h], ACT.Exp, bias=nbq[:, h:h + 1], scale=-1.0).then_inc(sem["eq_ready"], 1)

            def exp_w():
                act.wait_ge(sem["wmax_ready"], 1)
                for t in range(TT):
                    act.activation(pos[:, t], pos[:, t], ACT.Exp, bias=nwmax[:, t:t + 1]).then_inc(sem["ew_ready"], 1)
                act.wait_ge(sem["w1_in"], 16)
                act.activation(w1h[:], w1_raw[:], ACT.Copy).then_inc(sem["w1_hi"], 1)
                for j in range(TT):
                    act.wait_ge(sem["ew_T"], j + 1)
                    act.activation(ewTh[:, j], psum[4 + j % 2], ACT.Copy).then_inc(sem["ewT_hi"], 1)

            def ek_high(i):
                for j in range(TT):
                    act.wait_ge(sem["ek_T"], TT * i + j + 1)
                    act.activation(EKh[:, j], psum[6 + j % 2], ACT.Copy).then_inc(sem["EK_hi"], 1)

            def a_high(j):
                for h in range(DH):
                    act.wait_ge(sem["a_T"], DH * j + h + 1)
                    act.activation(aTh[:, h], psum[4 + h], ACT.Copy).then_inc(sem["aT_hi"], 1)

            def hidden(j):
                for m in range(HT):
                    act.wait_ge(sem["ffn1_done"], HT * j + m + 1)
                    act.activation(hT[:, m], psum[4 + m % 2], ACT.Relu,
                                   bias=b1c[:, m:m + 1]).then_inc(sem["h_ready"], 1)

            def z_high(j):
                act.wait_ge(sem["z_ready"], TT * (j + 1))
                act.activation(z16h[:, j], z_sb[:], ACT.Copy, scale=Z_SCALE).then_inc(sem["z16_hi"], 1)
                for h in range(DH):
                    act.wait_ge(sem["z_T"], DH * j + h + 1)
                    act.activation(zTh[:, h, j], psum[6 + h], ACT.Copy).then_inc(sem["zT_hi"], 1)

            def phi_high(n):
                act.wait_ge(sem["phi_in"], 16 * (n + 1))
                if reached(n, 2):
                    act.wait_ge(sem["l_full"], TT * (n - 1))
                for h in range(DH):
                    ins = act.activation(phih[:, n % 2, h].rearrange("p (g s e) -> p g e s", g=SUB, s=PE_),
                                         phi_by_slot(h), ACT.Copy)
                ins.then_inc(sem["phi_hi"], 1)

            act.wait_ge(sem["wqkv_in"], 48)
            act.activation(wqkvh[:], wqkv_raw[:], ACT.Copy).then_inc(sem["wqkv_hi"], 1)
            embedding_high(0)
            act.wait_ge(sem["nbq_ready"], 1)
            exp_kq(0)
            exp_w()
            ek_high(0)
            embedding_high(1)

            exp_kq(1)
            ek_high(1)
            a_high(0)
            hidden(0)
            embedding_high(2)
            with act.Fori(2, B) as i:
                exp_kq(i)
                ek_high(i)
                a_high(i - 1)
                hidden(i - 1)
                embedding_high(i + 1)
                z_high(i - 2)
            a_high(B - 1)
            hidden(B - 1)
            phi_high(0)
            z_high(B - 2)
            phi_high(1)
            z_high(B - 1)

            def dispatch_high(n, m):
                act.wait_ge(sem["d_ready"], TT * n + m + 1)
                if reached(n, 2):
                    act.wait_ge(sem["slots_done"], B * (n - 1))
                act.activation(disph[:, n % 2, m], ed[:, m % 2], ACT.Copy).then_inc(sem["disp_hi"], 1)

            def softmaxes(n, m):
                L = logits_ps[m % 2]
                act.wait_ge(sem["sub_ready"], TT * n + m + 1)
                act.activation(ed[:, m % 2], ed[:, m % 2], ACT.Exp).then_inc(sem["e_ready"], 1)
                act.wait_ge(sem["nmax_ready"], TT * n + m + 1)
                if reached(n):
                    act.wait_ge(sem["comb_T"], SUB * (TT * (n - 1) + m + 1))
                if reached(n):
                    act.wait_ge(sem["s_ready"], TT * (n - 1) + m + 1)
                for b in range(B):
                    ins = act.activation(e2[:, m, b], L[:, b], ACT.Exp, bias=nRn[:, m, b:b + 1],
                                         accum_out=csum[:, m, b:b + 1])
                ins.then_inc(sem["e2_ready"], 1)
                if reached(n, 2):
                    act.wait_ge(sem["acc_added"], 2 * (TT * (n - 2) + m + 1))
                act.activation(alpha[:, n % 2, m], dR[:, m], ACT.Exp).then_inc(sem["alpha_ready"], 1)

            def slots_out(c, b):
                act.wait_ge(sem["slots_done"], B * c + b + 1)
                if reached(c):
                    act.wait_ge(sem["y_done"], (CE // 2) * c)
                for h in range(DH):
                    ins = act.activation(slotsT[:, h, :, b, :].rearrange("p (g e) s -> p g s e", g=SUB),
                                         psum[4 + b % 2][:, h * CS:(h + 1) * CS].rearrange("p (g s e) -> p g s e", g=SUB, s=PE_),
                                         ACT.Copy, scale=1.0 / (Z_SCALE * D_SCALE))
                ins.then_inc(sem["slotsT_ready"], 1)

            def combine_out(n, m):
                for k in range(SUB):
                    act.wait_ge(sem["comb_T"], SUB * (TT * n + m) + k + 1)
                    act.activation(combT[:, k, :, m, :], psum[COMB_BANKS[m] + k].rearrange("p (b t) -> p b t", b=B),
                                   ACT.Copy).then_inc(sem["combT_ready"], 1)

            for m in range(TT):
                softmaxes(0, m)
                dispatch_high(0, m)
                if m < 2:
                    combine_out(0, m)
            softmaxes(1, 0)

            def step(c, n=None, after=None):
                slots_out(c, 0)
                combine_out(c, 2)
                if after is not None:
                    phi_high(after)
                if n is not None:
                    softmaxes(n, 1)
                slots_out(c, 1)
                slots_out(c, 2)
                combine_out(c, 3)
                slots_out(c, 3)
                if n is None:
                    return
                dispatch_high(n, 0)
                dispatch_high(n, 1)
                softmaxes(n, 2)
                softmaxes(n, 3)
                combine_out(n, 0)
                combine_out(n, 1)
                dispatch_high(n, 2)
                dispatch_high(n, 3)
                if after is not None:
                    softmaxes(after, 0)

            step(0, 1, 2)
            with act.Fori(1, CH - 2) as c:
                step(c, c + 1, c + 2)
            step(CH - 2, CH - 1)
            step(CH - 1)

        @block.vector
        def _(dve):
            def row(i):
                return rows[:, i:i + 1].broadcast_to([P, TT, D])

            def statistics(n, src, source, count, per_tile=0):
                for t in range(TT):
                    if t == 0 or per_tile:
                        dve.wait_ge(source, count + per_tile * t)
                    dve.bn_stats(st[n][:, t], src[:, t]).then_inc(dve_order, 1)
                    k = order.step()
                dve.wait_ge(dve_order, order.value(k))
                dve.memset(ve[n][:], EPS).then_inc(dve_order, 1)
                order.step()
                for t in range(TT):
                    dve.bn_aggr(mv[n][:, t], st[n][:, t]).then_inc(dve_order, 1)
                    last = order.step()
                dve.wait_ge(dve_order, order.value(last))
                dve.tensor_tensor(ve[n][:], mv[n][:, :, 1], ve[n][:], ALU.add).then_inc(var_ready[n], 1)

            def normalise(n, count, src, dst):
                dve.wait_ge(rstd_ready[n], count)
                for t in range(TT):
                    ins = dve.tensor_scalar(dst[:, t], src[:, t], mv[n][:, t, 0:1], rstd[n][:, t:t + 1],
                                            ALU.subtract, ALU.mult)
                    ins.then_inc(dve_order, 1)
                    k = order.step()
                return k

            def embedding_stats(made):
                statistics("x", xf, sem["x_in"], 16 * (made + 1))

            def embedding(made):
                if reached(made):
                    dve.wait_ge(sem["emb_T"], DH * made)
                if reached(made):
                    dve.wait_ge(sem["embb_made"], made)
                k = normalise("x", made + 1, xf, emb)
                dve.wait_ge(sem["ctx_arrived"], 16 * (made + 1))
                dve.wait_ge(dve_order, order.value(k))
                dve.tensor_tensor(emb[:], emb[:], ctxf[:], ALU.add).then_inc(sem["emb_ready"], 1)

            def embedding_low(i):
                for h in range(DH):
                    dve.wait_ge(sem["embT_hi"], DH * i + h + 1)
                    dve.tensor_tensor(embTl[:, h], psum[6 + h], embTh[:, h].bitcast(F32),
                                      ALU.subtract).then_inc(sem["embT_lo"], 1)

            def embedding_bias(i):
                dve.wait_ge(sem["emb_ready"], i + 1)
                dve.tensor_tensor(embb[:], emb[:], row(0), ALU.add).then_inc(sem["embb_made"], 1)

            def k_maxima(i):
                for h in range(DH):
                    dve.wait_ge(sem["qkv_done"], QKV * i + h + 1)
                    dve.tensor_reduce(km[:, h:h + 1], psum[h], AX_X, ALU.max).then_inc(dve_order, 1)
                    k = order.step()
                dve.wait_ge(dve_order, order.value(k))
                dve.tensor_tensor(kmb[:], km[:], cols[:, 1], ALU.add).then_inc(dve_order, 1)
                k = order.step()
                dve.wait_ge(dve_order, order.value(k))
                dve.tensor_tensor(kb[:], cols[:, 1], kmb[:], ALU.subtract).then_inc(sem["kb_ready"], 1)

            def ek_times_v(i):
                for h in range(DH):
                    dve.wait_ge(sem["qkv_done"], QKV * i + DH + h + 1)
                    dve.wait_ge(sem["ek_ready"], DH * i + h + 1)
                    dve.scalar_tensor_tensor(ekvT[:, h], psum[2 + h], cols[:, 2, h:h + 1], ekT[:, h],
                                             ALU.add, ALU.mult).then_inc(sem["ekv_ready"], 1)

            def ek_low(i):
                for j in range(TT):
                    dve.wait_ge(sem["EK_hi"], TT * i + j + 1)
                    dve.tensor_tensor(EKl[:, j], psum[6 + j % 2], EKh[:, j].bitcast(F32),
                                      ALU.subtract).then_inc(sem["EK_lo"], 1)

            def gate(i, h):
                    bank_den, bank_num = SUMS_BANKS[h]
                    dve.wait_ge(sem["sums_done"], 2 * (DH * i + h) + 1)
                    dve.wait_ge(sem["eq_ready"], DH * i + h + 1)
                    dve.scalar_tensor_tensor(yT[:, h], eq[:, h], 1.0, psum[bank_den], ALU.add, ALU.mult).then_inc(sem["den_read"], 1)
                    dve.wait_ge(sem["den_read"], DH * i + h + 1)
                    dve.reciprocal(yT[:, h], yT[:, h]).then_inc(dve_order, 1)
                    k = order.step()
                    dve.wait_ge(sem["sums_done"], 2 * (DH * i + h) + 2)
                    dve.wait_ge(dve_order, order.value(k))
                    dve.tensor_tensor(yT[:, h], psum[bank_num], yT[:, h], ALU.mult).then_inc(sem["y_ready"], 1)

            def attention_sum(j):
                dve.wait_ge(sem["embb_made"], j + 1)
                for t in range(TT):
                    dve.wait_ge(sem["attn_done"], TT * j + t + 1)
                    dve.tensor_tensor(a_sb[:, t], psum[6 + t % 2][:, 0:D], embb[:, t], ALU.add).then_inc(sem["s_added"], 1)
                statistics("a", a_sb, sem["s_added"], TT * j + 1, 1)

            def attention_norm(j):
                k = normalise("a", j + 1, a_sb, a_sb)
                dve.wait_ge(dve_order, order.value(k))
                dve.tensor_tensor(a_sb[:], a_sb[:], row(1), ALU.mult).then_inc(dve_order, 1)
                k = order.step()
                dve.wait_ge(dve_order, order.value(k))
                dve.tensor_tensor(a_sb[:], a_sb[:], row(2), ALU.add).then_inc(sem["a_ready"], 1)

            def attention_bias(j):
                dve.wait_ge(sem["a_ready"], j + 1)
                if reached(j):
                    dve.wait_ge(sem["z_ready"], TT * j)
                dve.wait_ge(sem["xb_in"], 16 * (j + 1))
                dve.tensor_tensor(ab2[:], a_sb[:], row(3), ALU.add).then_inc(dve_order, 1)
                return order.step()

            def a_low(j):
                for h in range(DH):
                    dve.wait_ge(sem["aT_hi"], DH * j + h + 1)
                    dve.tensor_tensor(aTl[:, h], psum[4 + h], aTh[:, h].bitcast(F32),
                                      ALU.subtract).then_inc(sem["aT_lo"], 1)

            def ffn_sum(j, t, k_ab2=None):
                if k_ab2 is not None:
                    dve.wait_ge(dve_order, order.value(k_ab2))
                dve.wait_ge(sem["ffn2_done"], TT * j + t + 1)
                dve.tensor_tensor(ab2[:, t], psum[4 + t % 2][:, 0:D], ab2[:, t], ALU.add).then_inc(sem["s2_added"], 1)

            def block_output(j):
                statistics("f", ab2, sem["s2_added"], TT * j + 1, 1)
                k = normalise("f", j + 1, ab2, ab2)
                dve.wait_ge(dve_order, order.value(k))
                dve.tensor_tensor(ab2[:], ab2[:], row(1), ALU.mult).then_inc(dve_order, 1)
                k = order.step()
                dve.wait_ge(dve_order, order.value(k))
                dve.tensor_tensor(ab2[:], ab2[:], row(2), ALU.add).then_inc(dve_order, 1)
                k = order.step()
                dve.wait_ge(sem["xb_in"], 16 * (j + 1))
                dve.wait_ge(dve_order, order.value(k))
                dve.tensor_tensor(ab2[:], ab2[:], xb[:], ALU.add).then_inc(sem["x1_ready"], 1)
                statistics("z", ab2, sem["x1_ready"], j + 1)
                dve.wait_ge(rstd_ready["z"], j + 1)
                for t in range(TT):
                    dve.tensor_scalar(z_sb[:, t], ab2[:, t], mv["z"][:, t, 0:1], rstd["z"][:, t:t + 1],
                                      ALU.subtract, ALU.mult).then_inc(sem["z_ready"], 1)

            def z_low(j):
                dve.wait_ge(sem["z16_hi"], j + 1)
                dve.scalar_tensor_tensor(z16l[:, j], z_sb[:], Z_SCALE, z16h[:, j],
                                         ALU.mult, ALU.subtract).then_inc(sem["z16_lo"], 1)
                for h in range(DH):
                    dve.wait_ge(sem["zT_hi"], DH * j + h + 1)
                    dve.tensor_tensor(zTl[:, h, j], psum[6 + h], zTh[:, h, j].bitcast(F32),
                                      ALU.subtract).then_inc(sem["zT_lo"], 1)

            def phi_low(n):
                dve.wait_ge(sem["phi_hi"], n + 1)
                for h in range(DH):
                    high, low = (t[:, n % 2, h].rearrange("p (g s e) -> p g e s", g=SUB, s=PE_) for t in (phih, phil))
                    ins = dve.tensor_tensor(low, phi_by_slot(h), high.bitcast(F32), ALU.subtract)
                ins.then_inc(sem["phi_lo"], 1)

            order = Order(0)
            embedding_stats(0)
            embedding(0)
            dve.wait_ge(sem["vectors_in"], 16 * 8)
            dve.tensor_scalar(nbq[:], cols[:, 0], -1.0, None, ALU.mult).then_inc(sem["nbq_ready"], 1)
            embedding_low(0)
            embedding_bias(0)
            k_maxima(0)
            ek_times_v(0)
            dve.wait_ge(sem["band_masked"], 1)
            dve.tensor_reduce(wmax[:], pos[:], AX_X, ALU.max).then_inc(dve_order, 1)
            k = order.step()
            dve.wait_ge(dve_order, order.value(k))
            dve.tensor_scalar(nwmax[:], wmax[:], -1.0, None, ALU.mult).then_inc(sem["wmax_ready"], 1)
            for j in range(TT):
                dve.wait_ge(sem["ewT_hi"], j + 1)
                dve.tensor_tensor(ewTl[:, j], psum[4 + j % 2], ewTh[:, j].bitcast(F32), ALU.subtract).then_inc(sem["ewT_lo"], 1)
            ek_low(0)
            embedding_stats(1)
            embedding(1)
            embedding_low(1)
            gate(0, 0)
            gate(0, 1)
            assert order.k == STEPS_A0, order.k

            def turn(i, end=True):
                attention_sum(i - 1)
                k_maxima(i)
                embedding_bias(i)
                ek_times_v(i)
                ek_low(i)
                attention_norm(i - 1)
                embedding_stats(i + 1)
                embedding(i + 1)
                a_low(i - 1)
                if end:
                    block_output(i - 2)
                embedding_low(i + 1)
                gate(i, 0)
                k_ab2 = attention_bias(i - 1)
                ffn_sum(i - 1, 0, k_ab2)
                if end:
                    z_low(i - 2)
                ffn_sum(i - 1, 1)
                gate(i, 1)
                ffn_sum(i - 1, 2)
                ffn_sum(i - 1, 3)

            order = Order(STEPS_A0)
            turn(1, end=False)
            assert order.k == STEPS_A1, order.k
            with dve.Fori(2, B) as i:
                order = Order(STEPS_A0 + STEPS_A1 + STEPS_A * (i - 2))
                turn(i)
                assert order.k == STEPS_A, order.k
            order = Order(STEPS_A0 + STEPS_A1 + STEPS_A * (B - 2))
            attention_sum(B - 1)
            attention_norm(B - 1)
            a_low(B - 1)
            block_output(B - 2)
            k_ab2 = attention_bias(B - 1)
            ffn_sum(B - 1, 0, k_ab2)
            z_low(B - 2)
            for t in range(1, TT):
                ffn_sum(B - 1, t)
            phi_low(0)
            block_output(B - 1)
            z_low(B - 1)
            assert order.k == STEPS_A2, order.k

            dve.wait_ge(sem["x1_spilled"], 16 * B)
            dve.wait_ge(sem["z16_lo"], B)
            dve.wait_ge(sem["zT_lo"], DH * B)
            dve.memset(S[:], 0.0).then_inc(sem["zeroed"], 1)
            dve.memset(nR[:], -LOWEST).then_inc(sem["zeroed"], 1)
            dve.wait_ge(sem["zeroed"], 2)

            def maxima(n, m):
                L = logits_ps[m % 2]
                dve.wait_ge(sem["l_full"], TT * n + m + 1)
                dve.tensor_reduce(cmax[:, m], L, AX_X, ALU.max).then_inc(dve_order, 1)
                k_c = order.step()
                dve.tensor_reduce(mx[:], L.rearrange("p b n -> p n b"), AX_X, ALU.max).then_inc(dve_order, 1)
                k_m = order.step()
                dve.wait_ge(dve_order, order.value(k_c))
                dve.scalar_tensor_tensor(nRn[:, m], cmax[:, m], -1.0, nR[:, m], ALU.mult, ALU.min).then_inc(dve_order, 1)
                k_r = order.step()
                if reached(n) or m >= 2:
                    dve.wait_ge(sem["disp_lo"], TT * n + m - 1)
                dve.wait_ge(dve_order, order.value(k_m))
                dve.tensor_tensor(ed[:, m % 2], L, mx[:].rearrange("p (a n) -> p a n", a=1).broadcast_to([P, B, CS]),
                                  ALU.subtract).then_inc(sem["sub_ready"], 1)
                dve.wait_ge(dve_order, order.value(k_r))
                dve.tensor_tensor(dR[:, m], nRn[:, m], nR[:, m], ALU.subtract).then_inc(sem["nmax_ready"], 1)
                dve.wait_ge(sem["nmax_ready"], TT * n + m + 1)
                dve.tensor_copy(nR[:, m], nRn[:, m]).then_inc(dve_order, 1)
                order.step()

            def dispatch(n, m):
                e = ed[:, m % 2]
                dve.wait_ge(sem["e_ready"], TT * n + m + 1)
                if reached(n) or m >= 1:
                    dve.wait_ge(sem["d_ready"], TT * n + m)
                dve.tensor_reduce(ssum[:], e.rearrange("p b n -> p n b"), AX_X, ALU.add).then_inc(dve_order, 1)
                k = order.step()
                dve.wait_ge(dve_order, order.value(k))
                dve.reciprocal(ssum[:], ssum[:]).then_inc(dve_order, 1)
                k = order.step()
                dve.wait_ge(dve_order, order.value(k))
                dve.scalar_tensor_tensor(e, e, D_SCALE, ssum[:].rearrange("p (a n) -> p a n", a=1).broadcast_to([P, B, CS]),
                                         ALU.mult, ALU.mult).then_inc(sem["d_ready"], 1)

            def add_bias(c, j):
                if j == 0:
                    dve.wait_ge(sem["eb_in"], 16 * (c + 1))
                    if reached(c):
                        for k in range(2):
                            dve.wait_ge(y_moved[k], 16 * SUB * (B // 2) * c)
                dve.wait_ge(sem["y_done"], (CE // 2) * c + j + 1)
                bank = psum[6 + j % 2].rearrange("p (n e) -> p n e", n=2)
                dve.tensor_tensor(y_sb[:, 2 * j:2 * j + 2], bank, ebb[:, 2 * j:2 * j + 2],
                                  ALU.add).then_inc(sem["y_ready_b"], 1)

            def accumulate(c, m):
                dve.wait_ge(sem["alpha_ready"], TT * c + m + 1)
                for k in range(2):
                    dve.wait_ge(sem["out_done"], 2 * (TT * c + m) + k + 1)
                    for q in range(2):
                        b = 2 * k + q
                        ins = dve.scalar_tensor_tensor(acc[:, b, m], acc[:, b, m], alpha[:, c % 2, m, b:b + 1],
                                                       psum[OUT_BANKS[m] + k][:, q * D:(q + 1) * D],
                                                       ALU.mult, ALU.add)
                    ins.then_inc(sem["acc_added"], 1)

            BASE_B = STEPS_A0 + STEPS_A1 + STEPS_A * (B - 2) + STEPS_A2
            order = Order(BASE_B)
            for m in range(TT):
                maxima(0, m)
                if m == 0:
                    phi_low(1)
                dispatch(0, m)
            maxima(1, 0)
            assert order.k == STEPS_B0, order.k

            def step(c, n=None, after=None):
                if n is None:
                    for j in range(CE // 2):
                        add_bias(c, j)
                    for m in range(TT):
                        accumulate(c, m)
                    return
                maxima(n, 1)
                dispatch(n, 0)
                if after is not None:
                    phi_low(after)
                dispatch(n, 1)
                for j in range(CE // 2):
                    add_bias(c, j)
                maxima(n, 2)
                maxima(n, 3)
                accumulate(c, 0)
                accumulate(c, 1)
                dispatch(n, 2)
                dispatch(n, 3)
                accumulate(c, 2)
                if after is not None:
                    maxima(after, 0)
                accumulate(c, 3)

            order = Order(BASE_B + STEPS_B0)
            dve.wait_ge(sem["acc_zeroed"], 1)
            step(0, 1, 2)
            assert order.k == STEPS_B, order.k
            with dve.Fori(1, CH - 2) as c:
                order = Order(BASE_B + STEPS_B0 + STEPS_B * c)
                step(c, c + 1, c + 2)
                assert order.k == STEPS_B, order.k
            order = Order(BASE_B + STEPS_B0 + STEPS_B * (CH - 2))
            step(CH - 2, CH - 1)
            step(CH - 1)
            dve.wait_ge(sem["s_ready"], TT * CH)
            dve.reciprocal(rS[:], S[:]).then_inc(sem["rS_ready"], 1)
            dve.wait_ge(sem["rS_ready"], 1)
            dve.wait_ge(sem["acc_added"], 2 * TT * CH)
            dve.wait_ge(sem["x1_back"], 16 * B)
            for b in range(B):
                for m in range(TT):
                    dve.scalar_tensor_tensor(acc[:, b, m], acc[:, b, m], rS[:, m, b:b + 1], x1_view[:, b, m],
                                             ALU.mult, ALU.add).then_inc(sem["out_ready"], 1)

        @block.tensor
        def _(pe):
            def split3(out_ap, Lh, Ll, Rh, Rl, start, stop):
                pe.matmul(out_ap, Lh, Rh, start=start, stop=False)
                pe.matmul(out_ap, Lh, Rl, start=False, stop=False)
                return pe.matmul(out_ap, Ll, Rh, start=False, stop=stop)

            def transposes(bank, sources):
                for q, src in enumerate(sources):
                    mm = pe.transpose(bank[:, q * P:(q + 1) * P], src, ident[:])
                return mm

            def t_emb(i):
                pe.wait_ge(sem["emb_ready"], i + 1)
                for h in range(DH):
                    if reached(i):
                        pe.wait_ge(sem["EK_lo"], TT * (i - 1) + 3 + h)
                    transposes(psum[6 + h], [emb[:, t, h * P:(h + 1) * P] for t in range(TT)]).then_inc(sem["emb_T"], 1)

            def qkv(i):
                pe.wait_ge(sem["embT_lo"], DH * (i + 1))
                for turn, w in enumerate((1, 2, 0)):
                    for e in range(DH):
                        bank = psum[(0, 2, 0)[turn] + e]
                        if turn == 2:
                            pe.wait_ge(sem["ek_ready"], DH * i + e + 1)
                        for h in range(DH):
                            mm = split3(bank, wqkvh[:, w, h, e * P:(e + 1) * P], wqkvl[:, w, h, e * P:(e + 1) * P],
                                        embTh[:, h], embTl[:, h], h == 0, h == DH - 1)
                        mm.then_inc(sem["qkv_done"], 1)

            def t_ek(i):
                pe.wait_ge(sem["ekv_ready"], DH * (i + 1))
                for j in range(TT):
                    if j < 2 and reached(i):
                        pe.wait_ge(sem["s_added"], TT * (i - 1) + 3 + j)
                    elif j < 2:
                        pe.wait_ge(sem["embT_lo"], DH * i + j + 1)
                    else:
                        pe.wait_ge(sem["EK_lo"], TT * i + j - 1)
                    transposes(psum[6 + j % 2], [src[:, h, j * P:(j + 1) * P] for src in (ekT, ekvT)
                                                 for h in range(DH)]).then_inc(sem["ek_T"], 1)

            def aft(i, h):
                if h == 0:
                    pe.wait_ge(sem["EK_lo"], TT * (i + 1))
                if True:
                    for kind in range(2):
                        bank = psum[SUMS_BANKS[h][kind]]
                        if h == 0:
                            pe.wait_ge(sem["ekv_ready"], DH * i + kind + 1)
                        else:
                            pe.wait_ge(sem["eq_ready"], DH * i + kind + 1)
                        c0 = kind * D + h * P
                        for j in range(TT):
                            mm = split3(bank, EKh[:, j, c0:c0 + P], EKl[:, j, c0:c0 + P], ewTh[:, j], ewTl[:, j],
                                        j == 0, j == TT - 1)
                        mm.then_inc(sem["sums_done"], 1)

            def attention(j):
                pe.wait_ge(sem["y_ready"], DH * (j + 1))
                for t in range(TT):
                    bank = psum[6 + t % 2]
                    if t >= 2:
                        pe.wait_ge(sem["s_added"], TT * j + t - 1)
                    for h in range(DH):
                        mm = pe.matmul(bank[:, 0:D], yT[:, h, t * P:(t + 1) * P], wo_sb[:, h],
                                       start=(h == 0), stop=(h == DH - 1))
                    mm.then_inc(sem["attn_done"], 1)

            def t_a(j):
                pe.wait_ge(sem["a_ready"], j + 1)
                for h in range(DH):
                    transposes(psum[4 + h], [a_sb[:, t, h * P:(h + 1) * P] for t in range(TT)]).then_inc(sem["a_T"], 1)

            def ffn1(j):
                pe.wait_ge(sem["aT_lo"], DH * (j + 1))
                for m in range(HT):
                    bank = psum[4 + m % 2]
                    if m >= 2:
                        pe.wait_ge(sem["h_ready"], HT * j + m - 1)
                    for h in range(DH):
                        mm = split3(bank, w1h[:, h, m * P:(m + 1) * P], w1l[:, h, m * P:(m + 1) * P],
                                    aTh[:, h], aTl[:, h], h == 0, h == DH - 1)
                    mm.then_inc(sem["ffn1_done"], 1)

            def ffn2(j, tiles):
                for t in tiles:
                    bank = psum[4 + t % 2]
                    if t >= 2:
                        pe.wait_ge(sem["s2_added"], TT * j + t - 1)
                    else:
                        pe.wait_ge(sem["h_ready"], HT * j + HT - 1 + t)
                    for m in range(HT):
                        if t == 0:
                            pe.wait_ge(sem["h_ready"], HT * j + m + 1)
                        mm = pe.matmul(bank[:, 0:D], hT[:, m, t * P:(t + 1) * P], w2_sb[:, m],
                                       start=(m == 0), stop=(m == HT - 1))
                    mm.then_inc(sem["ffn2_done"], 1)

            def t_z(j):
                pe.wait_ge(sem["z_ready"], TT * (j + 1))
                for h in range(DH):
                    if isinstance(j, int) and j == B - 1:
                        pe.wait_ge(sem["zT_lo"], DH * (j - 1) + h + 1)
                    elif isinstance(j, int) and j == B - 2:
                        pe.wait_ge(sem["s_added"], TT * (B - 1) + 3 + h)
                    else:
                        pe.wait_ge(sem["embT_lo"], DH * (j + 3) + h + 1)
                    transposes(psum[6 + h], [z_sb[:, t, h * P:(h + 1) * P] for t in range(TT)]).then_inc(sem["z_T"], 1)

            pe.wait_ge(sem["ident_made"], 1)
            t_emb(0)
            pe.wait_ge(sem["wqkv_lo"], 1)
            qkv(0)
            pe.wait_ge(sem["ew_ready"], TT)
            for j in range(TT):
                if j >= 2:
                    pe.wait_ge(sem["ewT_lo"], j - 1)
                for t in range(TT):
                    mm = pe.transpose(psum[4 + j % 2][:, t * P:(t + 1) * P], pos[:, t, j * P:(j + 1) * P], ident[:])
                mm.then_inc(sem["ew_T"], 1)
            t_ek(0)
            pe.wait_ge(sem["ewT_lo"], TT)
            aft(0, 0)
            aft(0, 1)
            t_emb(1)
            pe.wait_ge(sem["wo_w2_in"], 32)

            def turn(i, end=True):
                attention(i - 1)
                qkv(i)
                t_ek(i)
                aft(i, 0)
                t_a(i - 1)
                aft(i, 1)
                if not end:
                    pe.wait_ge(sem["w1_lo"], 1)
                ffn1(i - 1)
                t_emb(i + 1)
                ffn2(i - 1, [0])
                if end:
                    t_z(i - 2)
                ffn2(i - 1, range(1, TT))

            turn(1, end=False)
            with pe.Fori(2, B) as i:
                turn(i)
            attention(B - 1)
            t_a(B - 1)
            ffn1(B - 1)
            ffn2(B - 1, [0])
            t_z(B - 2)
            ffn2(B - 1, range(1, TT))
            t_z(B - 1)

            def logits(n, m):
                if m == 0:
                    pe.wait_ge(sem["phi_lo"], n + 1)
                if reached(n) or m >= 2:
                    pe.wait_ge(sem["e2_ready"], TT * n + m - 1)
                for b in range(B):
                    for h in range(DH):
                        mm = split3(logits_ps[m % 2][:, b], zTh[:, h, b, m * P:(m + 1) * P], zTl[:, h, b, m * P:(m + 1) * P],
                                    phih[:, n % 2, h], phil[:, n % 2, h], h == 0, h == DH - 1)
                mm.then_inc(sem["l_full"], 1)

            def t_combine(n, m):
                pe.wait_ge(sem["e2_ready"], TT * n + m + 1)
                for k in range(SUB):
                    if m == 3:
                        pe.wait_ge(sem["combT_ready"], SUB * (TT * n + 2) + k + 1)
                    elif m == 2 and reached(n):
                        pe.wait_ge(sem["acc_added"], 2 * (TT * (n - 1) + 3) + k + 1)
                    elif m == 2:
                        pe.wait_ge(sem["combT_ready"], SUB + k + 1)
                    elif reached(n):
                        pe.wait_ge(sem["acc_added"], 2 * (TT * (n - 1) + m) + k + 1)
                    transposes(psum[COMB_BANKS[m] + k],
                               [e2[:, m, b, k * P:(k + 1) * P] for b in range(B)]).then_inc(sem["comb_T"], 1)

            def slots(c, b):
                if b == 0:
                    pe.wait_ge(sem["disp_lo"], TT * (c + 1))
                bank = psum[4 + b % 2]
                if b >= 2:
                    pe.wait_ge(sem["slotsT_ready"], B * c + b - 1)
                elif reached(c):
                    pe.wait_ge(sem["acc_added"], 2 * (TT * (c - 1) + 2) + b + 1)
                else:
                    pe.wait_ge(sem["combT_ready"], b + 1)
                for h in range(DH):
                    for m in range(TT):
                        hs = slice(h * P, (h + 1) * P)
                        mm = split3(bank[:, h * CS:(h + 1) * CS], z16h[:, b, m, hs], z16l[:, b, m, hs],
                                    disph[:, c % 2, m, b], displ[:, c % 2, m, b], m == 0, m == TT - 1)
                mm.then_inc(sem["slots_done"], 1)

            def experts(c):
                pe.wait_ge(sem["slotsT_ready"], B * (c + 1))
                for j in range(CE // 2):
                    bank = psum[6 + j % 2]
                    if j >= 2:
                        pe.wait_ge(sem["y_ready_b"], (CE // 2) * c + j - 1)
                    else:
                        pe.wait_ge(sem["combT_ready"], SUB * TT * (c + 1) - 1 + j)
                    if j % 2 == 0:
                        pe.wait_ge(W_in[j // 2], 16 * (c + 1))
                    for q in range(2):
                        for h in range(DH):
                            mm = pe.matmul(bank[:, q * D:(q + 1) * D],
                                           slotsT[:, h, 2 * j + q].rearrange("p b s -> p (b s)"), Wr[:, 2 * j + q, h],
                                           start=(h == 0), stop=(h == DH - 1))
                    mm.then_inc(sem["y_done"], 1)

            def combine(c, m, n):
                if m == 0:
                    pe.wait_ge(sem["combT_ready"], SUB * TT * (c + 1))
                for k in range(2):
                    bank = psum[OUT_BANKS[m] + k]
                    if m == 0:
                        pe.wait_ge(y_moved[k], 16 * SUB * (B // 2) * (c + 1))
                        pe.wait_ge(sem["slotsT_ready"], B * c + 2 + k + 1)
                    elif m == 1:
                        pe.wait_ge(sem["y_ready_b"], (CE // 2) * c + 2 + k + 1)
                    elif n is not None:
                        pe.wait_ge(sem["combT_ready"], SUB * (TT * n + m - 2) + k + 1)
                    else:
                        pe.wait_ge(sem["acc_added"], 2 * (TT * c + m - 2) + k + 1)
                    for q in range(2):
                        b = 2 * k + q
                        for u in range(SUB):
                            mm = pe.matmul(bank[:, q * D:(q + 1) * D], combT[:, u, b, m], y_c[:, u, b],
                                           start=(u == 0), stop=(u == SUB - 1))
                    mm.then_inc(sem["out_done"], 1)

            pe.wait_ge(sem["zT_lo"], DH * B)
            logits(0, 0)
            logits(0, 1)
            t_combine(0, 0)
            logits(0, 2)
            t_combine(0, 1)
            logits(0, 3)
            logits(1, 0)
            logits(1, 1)

            def step(c, n=None, after=None):
                slots(c, 0)
                t_combine(c, 2)
                slots(c, 1)
                slots(c, 2)
                t_combine(c, 3)
                slots(c, 3)
                experts(c)
                if n is not None:
                    logits(n, 2)
                    logits(n, 3)
                combine(c, 0, n)
                combine(c, 1, n)
                if after is not None:
                    logits(after, 0)
                if n is not None:
                    t_combine(n, 0)
                    t_combine(n, 1)
                combine(c, 2, n)
                if after is not None:
                    logits(after, 1)
                combine(c, 3, n)

            step(0, 1, 2)
            with pe.Fori(1, CH - 2) as c:
                step(c, c + 1, c + 2)
            step(CH - 2, CH - 1)
            step(CH - 1)


_INS = ["x", "ctx_1024", "L0_xattn_wq", "L0_xattn_bq", "L0_xattn_wk", "L0_xattn_bk", "L0_xattn_wv", "L0_xattn_bv",
        "L0_xattn_wo", "L0_xattn_bo", "L0_xattn_pos_bias", "L0_xattn_gamma", "L0_xattn_beta", "L0_xattn_w1",
        "L0_xattn_b1", "L0_xattn_w2", "L0_xattn_b2", "L0_ffn_phi", "L0_ffn_W", "L0_ffn_b"]
_OUTS = [((4, 512, 256), "float32")]


def kernel(**inputs):
    import numpy as _np
    import concourse.bacc as _bacc
    from concourse import mybir as _mybir
    from concourse.bass_utils import run_bass_kernel_spmd as _run

    nc = _bacc.Bacc("TRN2", target_bir_lowering=False, num_devices=1)
    arrays, args = {}, []
    for name in _INS:
        a = _np.ascontiguousarray(inputs[name])
        arrays[f"in_{name}_dram"] = a
        args.append(nc.dram_tensor(f"in_{name}_dram", a.shape, _mybir.dt.from_np(a.dtype), kind="ExternalInput").ap())
    for i, (shape, dtype) in enumerate(_OUTS):
        dt = _mybir.dt.from_np(_np.dtype(dtype))
        args.append(nc.dram_tensor(f"out_{i}_dram", shape, dt, kind="ExternalOutput").ap())
    bass_aft_soft_moe(nc, *args)
    r = _run(nc, [arrays], core_ids=[0])
    return r.results[0]["out_0_dram"]
```

```python
from contextlib import ExitStack

import concourse.bass as bass
from concourse import mybir

F32 = mybir.dt.float32
F32R = mybir.dt.float32r
F16 = mybir.dt.float16
ALU = mybir.AluOpType
ACT = mybir.ActivationFunctionType
AX_X = mybir.AxisListType.X


def reached(n, first=1):
    return not isinstance(n, int) or n >= first


class Order:

    def __init__(self, base):
        self.base, self.k = base, 0

    def step(self):
        self.k += 1
        return self.k

    def value(self, k):
        return self.base + k


def bass_aft_soft_moe(nc, x, ctx_in, wq, bq, wk, bk, wv, bv, wo, bo, pos_bias, gamma, beta,
                      w1, b1, w2, b2, phi, W, eb, out):
    P = 128
    B, T, D = x.shape
    H = w1.shape[1]
    NE, _, PE_ = phi.shape[1], phi.shape[0], phi.shape[2]
    TT = T // P
    DH = D // P
    HT = H // P
    CE = 8
    CS = CE * PE_
    CH = NE // CE
    SUB = CS // P
    EPS = 1e-5
    BAND = 64
    Z_SCALE = 256.0
    D_SCALE = 4096.0
    LOWEST = -3.0e38
    QKV = 3 * DH
    LAST_TILES = (("sum", 0), ("f", 0), ("sum", 1), ("f", 1), ("z", 0), ("sum", 2), ("f", 2), ("z", 1), ("end", 0),
                  ("sum", 3), ("f", 3), ("z", 2), ("end", 1), ("z", 3), ("end", 2), ("end", 3))
    OUT_BANKS = (4, 6, 4, 6)
    EK_BANKS = (6, 7, 0, 1)
    COMB_BANKS = (4, 6, 6, 6)
    SUMS_BANKS = ((2, 3), (0, 1))
    STEPS_A0, STEPS_A1, STEPS_A, STEPS_A2, STEPS_B0, STEPS_B = 32, 32, 54, 64, 24, 20
    assert B * PE_ == P and SUB == 2 and DH == 2 and TT == 4

    x_d = x.rearrange("b (t p) d -> b p t d", p=P)
    ctx_d = ctx_in.rearrange("b (t p) d -> b p t d", p=P)
    out_d = out.rearrange("b (t p) d -> b p t d", p=P)
    phi_d = phi.rearrange("(h p) (c n) s -> c p h (n s)", p=P, n=CE)
    eb_d = eb.rearrange("(c n) e -> c (n e)", n=CE)
    W_d = W.rearrange("(c n) (h p) e -> c p n h e", p=P, n=CE)
    spill = nc.dram_tensor("x1_spill", (B, T, D), F32, kind="Internal").ap()
    spill_d = spill.rearrange("b (t p) d -> b p t d", p=P)

    with ExitStack() as stack:
        def sb(name, shape, dt, where=stack):
            return where.enter_context(nc.sbuf_tensor(name, shape, dt))

        logits_ps = [stack.enter_context(nc.psum_tensor(f"ps_pair{i}", [P, B, CS], F32))[:, :, :] for i in range(2)]
        psum = [logits_ps[k // 2][:, 2 * (k % 2):2 * (k % 2) + 2, :].rearrange("p a n -> p (a n)") for k in range(4)]
        psum += [stack.enter_context(nc.psum_tensor(f"ps{k}", [P, 512], F32))[:, :] for k in range(4, 8)]

        ident = sb("ident", [P, P], F32)
        zTh = sb("zTh", [P, DH, B, T], F32R)
        zTl = sb("zTl", [P, DH, B, T], F32R)
        z16h = sb("z16h", [P, B, TT, D], F16)
        z16l = sb("z16l", [P, B, TT, D], F16)

        stage_a = ExitStack()
        ewTh = sb("ewTh", [P, TT, T], F32R, stage_a)
        ewTl = sb("ewTl", [P, TT, T], F32R, stage_a)
        EKh = sb("EKh", [P, TT, 2 * D], F32R, stage_a)
        EKl = sb("EKl", [P, TT, 2 * D], F32R, stage_a)
        wqkvh = sb("wqkvh", [P, 3, DH, D], F32R, stage_a)
        wqkvl = sb("wqkvl", [P, 3, DH, D], F32R, stage_a)
        setup = ExitStack()
        pos = sb("pos", [P, TT, T], F32, setup)
        wqkv_raw = sb("wqkv_raw", [P, 3, DH, D], F32, setup)
        w1_raw = sb("w1_raw", [P, DH, H], F32, setup)
        setup.close()
        hT = sb("hT", [P, HT, T], F32, stage_a)
        aTh = sb("aTh", [P, DH, T], F32R, stage_a)
        aTl = sb("aTl", [P, DH, T], F32R, stage_a)
        xf = sb("xf", [P, TT, D], F32, stage_a)
        ctxf = sb("ctxf", [P, TT, D], F32, stage_a)
        emb = sb("emb", [P, TT, D], F32, stage_a)
        embb = sb("embb", [P, TT, D], F32, stage_a)
        embTh = sb("embTh", [P, DH, T], F32R, stage_a)
        embTl = sb("embTl", [P, DH, T], F32R, stage_a)
        wo_sb = sb("wo_sb", [P, DH, D], F32, stage_a)
        w1h = sb("w1h", [P, DH, H], F32R, stage_a)
        w1l = sb("w1l", [P, DH, H], F32R, stage_a)
        w2_sb = sb("w2_sb", [P, HT, D], F32, stage_a)
        rows = sb("rows", [P, 4, D], F32, stage_a)
        cols = sb("cols", [P, 3, DH], F32, stage_a)
        nbq = sb("nbq", [P, DH], F32, stage_a)
        b1c = sb("b1c", [P, HT], F32, stage_a)
        km = sb("km", [P, DH], F32, stage_a)
        kmb = sb("kmb", [P, DH], F32, stage_a)
        kb = sb("kb", [P, DH], F32, stage_a)
        wmax = sb("wmax", [P, TT], F32, stage_a)
        nwmax = sb("nwmax", [P, TT], F32, stage_a)
        mhalf = sb("mhalf", [P, TT], F32, stage_a)
        LN = ("x", "a", "f", "z")
        st = {n: sb(f"st_{n}", [P, TT, 6], F32, stage_a) for n in LN}
        mv = {n: sb(f"mv_{n}", [P, TT, 2], F32, stage_a) for n in LN}
        ve = {n: sb(f"ve_{n}", [P, TT], F32, stage_a) for n in LN}
        rstd = {n: sb(f"rstd_{n}", [P, TT], F32, stage_a) for n in LN}
        a_sb = sb("a_sb", [P, TT, D], F32, stage_a)
        ab2 = sb("ab2", [P, TT, D], F32, stage_a)
        xb = sb("xb", [P, TT, D], F32, stage_a)
        z_sb = sb("z_sb", [P, TT, D], F32, stage_a)
        eq = sb("eq", [P, DH, T], F32, stage_a)
        ekT = sb("ekT", [P, DH, T], F32, stage_a)
        ekvT = sb("ekvT", [P, DH, T], F32, stage_a)
        yT = sb("yT", [P, DH, T], F32, stage_a)
        stage_a.close()

        Wr = sb("Wr", [P, CE, DH, D], F32)
        phi_raw = sb("phi_raw", [P, DH, CS], F32)
        phih = sb("phih", [P, 2, DH, CS], F32R)
        phil = sb("phil", [P, 2, DH, CS], F32R)
        ebb = sb("ebb", [P, CE, D], F32)
        slotsT = sb("slotsT", [P, DH, CE, B, PE_], F32)
        acc = sb("acc", [P, B, TT, D], F32)
        disph = sb("disph", [P, TT, B, CS], F16)
        displ = sb("displ", [P, TT, B, CS], F16)
        e2 = sb("e2", [P, TT, B, CS], F32)
        combT = sb("combT", [P, SUB, B, TT, P], F32)
        y_sb = sb("y_sb", [P, CE, D], F32)
        y_c = sb("y_c", [P, SUB, B, D], F32)
        mx = sb("mx", [P, CS], F32)
        ed = sb("ed", [P, TT, B, CS], F32)
        s01 = sb("s01", [P, 2, CS], F32)
        ssum = sb("ssum", [P, 2, CS], F32)
        cmax = sb("cmax", [P, TT, B], F32)
        nR = sb("nR", [P, TT, B], F32)
        nRn = sb("nRn", [P, TT, B], F32)
        dR = sb("dR", [P, TT, B], F32)
        alpha = sb("alpha", [P, 2, TT, B], F32)
        csum = sb("csum", [P, TT, B], F32)
        S = sb("S", [P, TT, B], F32)
        rS = sb("rS", [P, TT, B], F32)

        def phi_by_slot(h):
            return phi_raw[:, h].rearrange("p (g e s) -> p g e s", g=SUB, s=PE_)

        x1_view = Wr[:].rearrange("p (b t) h e -> p b (t h) e", b=B)

        names = """ident_made consts_made band_masked x_in ctx_arrived xb_in xb_ready wqkv_in w1_in pos_in vectors_in
            wo_w2_in pool_order dve_order wqkv_hi w1_hi wqkv_lo w1_lo wmax_ready ew_ready ew_T ewT_hi ewT_lo
            nbq_ready emb_ready embb_made emb_T embT_hi embT_lo qkv_done kb_ready ek_ready eq_ready
            ekv_ready ek_T EK_hi EK_lo sums_done den_read y_ready attn_done s_added a_ready a_T aT_hi aT_lo
            ffn1_done h_ready ffn2_done s2_added x1_ready x1_spilled z_ready z_T z16_hi z16_lo zT_hi zT_lo
            phi_in phi_hi phi_lo eb_in l_full nmax_ready sub_ready e_ready d_ready disp_hi disp_lo
            e2_ready alpha_ready slots_done slotsT_ready y_done y_ready_b comb_T combT_ready
            out_done acc_added s_scaled s_ready rS_ready s01_ready ssum_ready x1_back out_ready out_stored zeroed
            acc_zeroed""".split()
        sem = {n: stack.enter_context(nc.semaphore(n)) for n in names}
        dve_order = sem["dve_order"]
        var_ready = {n: stack.enter_context(nc.semaphore(f"var_ready_{n}")) for n in LN}
        rstd_ready = {n: stack.enter_context(nc.semaphore(f"rstd_ready_{n}")) for n in LN}
        y_moved = [stack.enter_context(nc.semaphore(f"y_moved{k}")) for k in range(2)]
        W_in = [stack.enter_context(nc.semaphore(f"W_in{g}")) for g in range(2)]

        block = stack.enter_context(nc.Block())

        @block.sync
        def _(sp):
            sp.dma_start(xf[:], x_d[0]).then_inc(sem["x_in"], 16)
            for i, w in enumerate((wq, wk, wv)):
                sp.dma_start(wqkv_raw[:, i], w.rearrange("(h p) e -> p h e", p=P)).then_inc(sem["wqkv_in"], 16)
            sp.dma_start(ctxf[:], ctx_d[0]).then_inc(sem["ctx_arrived"], 16)
            sp.dma_start(pos[:], pos_bias.rearrange("(t p) j -> p t j", p=P)).then_inc(sem["pos_in"], 16)
            for i, v in enumerate((bq, bk, bv)):
                sp.dma_start(cols[:, i, :], v.rearrange("(h p) -> p h", p=P),
                             allow_slow_non_contiguous=True).then_inc(sem["vectors_in"], 16)
            for i, v in enumerate((bo, gamma, beta, b2)):
                sp.dma_start(rows[:, i, :],
                             v.rearrange("(a d) -> a d", a=1).broadcast_to([P, D])).then_inc(sem["vectors_in"], 16)
            sp.dma_start(b1c[:], b1.rearrange("(h p) -> p h", p=P),
                         allow_slow_non_contiguous=True).then_inc(sem["vectors_in"], 16)
            sp.dma_start(w1_raw[:], w1.rearrange("(h p) e -> p h e", p=P)).then_inc(sem["w1_in"], 16)
            sp.dma_start(wo_sb[:], wo.rearrange("(h p) e -> p h e", p=P)).then_inc(sem["wo_w2_in"], 16)
            sp.dma_start(w2_sb[:], w2.rearrange("(h p) e -> p h e", p=P)).then_inc(sem["wo_w2_in"], 16)

            def batch(d, b):
                return d[b] if isinstance(b, int) else d[bass.ds(b, 1)].rearrange("a p t d -> (a p) t d")

            def load_front(b, made):
                sp.wait_ge(sem["emb_ready"], made)
                sp.dma_start(xf[:], batch(x_d, b)).then_inc(sem["x_in"], 16)
                sp.dma_start(ctxf[:], batch(ctx_d, b)).then_inc(sem["ctx_arrived"], 16)

            def load_back(j):
                if reached(j):
                    sp.wait_ge(sem["x1_ready"], j)
                sp.dma_start(xb[:], batch(x_d, j)).then_inc(sem["xb_in"], 16)

            def store_back(j):
                sp.wait_ge(sem["x1_ready"], j + 1)
                sp.dma_start(batch(spill_d, j), ab2[:]).then_inc(sem["x1_spilled"], 16)

            load_front(1, 1)
            load_back(0)
            load_front(2, 2)
            with sp.Fori(2, B) as i:
                load_front((i + 1) % B, i + 1)
                store_back(i - 2)
                sp.wait_ge(sem["x1_spilled"], 16 * (i - 1))
                load_back(i - 1)
            store_back(B - 2)
            sp.wait_ge(sem["x1_spilled"], 16 * (B - 1))
            load_back(B - 1)

            def load_phi(c):
                if reached(c):
                    sp.wait_ge(sem["phi_lo"], c)
                src = phi_d[c] if isinstance(c, int) else phi_d[bass.ds(c, 1)].rearrange("a p h s -> (a p) h s")
                sp.dma_start(phi_raw[:], src).then_inc(sem["phi_in"], 16)

            def load_experts(c):
                src = W_d[c] if isinstance(c, int) else W_d[bass.ds(c, 1)].rearrange("a p n h e -> (a p) n h e")
                for g in range(2):
                    if reached(c):
                        sp.wait_ge(sem["y_done"], (CE // 2) * (c - 1) + 2 * g + 2)
                    sp.dma_start(Wr[:, 4 * g:4 * g + 4], src[:, 4 * g:4 * g + 4]).then_inc(W_in[g], 16)
                bias = eb_d[c:c + 1] if isinstance(c, int) else eb_d[bass.ds(c, 1)]
                if reached(c):
                    sp.wait_ge(sem["out_done"], 2 * TT * c)
                sp.dma_start(ebb[:].rearrange("p n e -> p (n e)"),
                             bias.broadcast_to([P, CE * D])).then_inc(sem["eb_in"], 16)

            def move_y(c):
                for g in range(SUB):
                    sp.wait_ge(sem["y_ready_b"], (CE // 2) * c + 2 * g + 2)
                    for b in range(B):
                        sp.dma_start(y_c[:, g, b, :],
                                     y_sb[PE_ * b:PE_ * (b + 1), 4 * g:4 * g + 4, :]).then_inc(y_moved[b // 2], 16)

            sp.wait_ge(sem["sums_done"], 2 * DH * B)
            load_phi(0)
            load_experts(0)
            load_phi(1)
            sp.wait_ge(sem["x1_ready"], B - 1 + TT)
            sp.dma_start(spill_d[B - 1], ab2[:]).then_inc(sem["x1_spilled"], 16)
            load_phi(2)
            move_y(0)
            with sp.Fori(1, CH - 2) as c:
                load_phi(c + 2)
                load_experts(c)
                move_y(c)
            for c in (CH - 2, CH - 1):
                load_experts(c)
                move_y(c)
            sp.wait_ge(sem["y_done"], (CE // 2) * CH)
            for b in range(B):
                sp.dma_start(x1_view[:, b], spill_d[b]).then_inc(sem["x1_back"], 16)
            for m in range(TT):
                sp.wait_ge(sem["out_ready"], m + 1)
                for b in range(B):
                    sp.dma_start(out_d[b][:, m], acc[:, b, m]).then_inc(sem["out_stored"], 16)
            sp.wait_ge(sem["out_stored"], 16 * B * TT)

        @block.gpsimd
        def _(pool):
            pool.memset(ident[:], 0.0).then_inc(sem["pool_order"], 1)
            pool.wait_ge(sem["pool_order"], 1)
            pool.affine_select(out=ident[:], in_=ident[:], compare_op=ALU.not_equal, fill=1.0, base=0,
                               pattern=[[-1, P]], channel_multiplier=1).then_inc(sem["ident_made"], 1)
            pool.memset(mhalf[:], -0.5).then_inc(sem["consts_made"], 1)
            pool.wait_ge(sem["consts_made"], 1)

            def inverse_deviation(n, count):
                pool.wait_ge(var_ready[n], count)
                pool.tensor_tensor(rstd[n][:], ve[n][:], mhalf[:], ALU.pow).then_inc(rstd_ready[n], 1)

            inverse_deviation("x", 1)
            pool.wait_ge(sem["pos_in"], 16)
            pool.affine_select(out=pos[:], in_=pos[:], compare_op=ALU.is_ge, fill=0.0, base=BAND - 1,
                               pattern=[[P, TT], [-1, T]], channel_multiplier=1).then_inc(sem["pool_order"], 1)
            pool.wait_ge(sem["pool_order"], 2)
            pool.affine_select(out=pos[:], in_=pos[:], compare_op=ALU.is_ge, fill=0.0, base=BAND - 1,
                               pattern=[[-P, TT], [1, T]], channel_multiplier=-1).then_inc(sem["band_masked"], 1)

            inverse_deviation("x", 2)
            pool.wait_ge(sem["w1_hi"], 1)
            pool.tensor_tensor(w1l[:], w1_raw[:], w1h[:].bitcast(F32), ALU.subtract).then_inc(sem["w1_lo"], 1)

            def add_beta(j):
                pool.wait_ge(sem["xb_in"], 16 * (j + 1))
                pool.tensor_tensor(xb[:], xb[:], rows[:, 2:3].broadcast_to([P, TT, D]),
                                   ALU.add).then_inc(sem["xb_ready"], 1)

            inverse_deviation("a", 1)
            inverse_deviation("x", 3)
            add_beta(0)
            with pool.Fori(2, B) as i:
                inverse_deviation("a", i)
                inverse_deviation("x", i + 2)
                inverse_deviation("f", i - 1)
                inverse_deviation("z", i - 1)
                add_beta(i - 1)
            inverse_deviation("a", B)
            inverse_deviation("f", B - 1)
            inverse_deviation("z", B - 1)
            add_beta(B - 1)
            for n, t in LAST_TILES:
                if n in ("f", "z"):
                    pool.wait_ge(var_ready[n], B + t)
                    pool.tensor_tensor(rstd[n][:, t:t + 1], ve[n][:, t:t + 1], mhalf[:, t:t + 1],
                                       ALU.pow).then_inc(rstd_ready[n], 1)

            pool.wait_ge(sem["ffn2_done"], TT * B)
            pool.memset(acc[:], 0.0).then_inc(sem["acc_zeroed"], 1)
            pool.wait_ge(sem["zeroed"], 2)

            def batch_sum(n, m):
                e = ed[:, m]
                pool.wait_ge(sem["e_ready"], TT * n + m + 1)
                pool.tensor_tensor(s01[:], e[:, 0:2], e[:, 2:4], ALU.add).then_inc(sem["s01_ready"], 1)
                pool.wait_ge(sem["s01_ready"], TT * n + m + 1)
                pool.tensor_tensor(ssum[:, m % 2], s01[:, 0], s01[:, 1], ALU.add).then_inc(sem["ssum_ready"], 1)

            def rescale_sum(n, m):
                pool.wait_ge(sem["alpha_ready"], TT * n + m + 1)
                if reached(n) or m >= 1:
                    pool.wait_ge(sem["s_ready"], TT * n + m)
                pool.tensor_tensor(S[:, m], S[:, m], alpha[:, n % 2, m], ALU.mult).then_inc(sem["s_scaled"], 1)
                pool.wait_ge(sem["s_scaled"], TT * n + m + 1)
                pool.tensor_tensor(S[:, m], S[:, m], csum[:, m], ALU.add).then_inc(sem["s_ready"], 1)

            def dispatch_low(n, m):
                pool.wait_ge(sem["disp_hi"], TT * n + m + 1)
                pool.tensor_tensor(displ[:, m], ed[:, m], disph[:, m], ALU.subtract).then_inc(sem["disp_lo"], 1)

            def softmaxes(n):
                for m in (0, 1):
                    batch_sum(n, m)
                    rescale_sum(n, m)
                for m in (0, 1):
                    dispatch_low(n, m)
                for m in (2, 3):
                    batch_sum(n, m)
                    rescale_sum(n, m)
                for m in (2, 3):
                    dispatch_low(n, m)

            for m in range(TT):
                batch_sum(0, m)
                rescale_sum(0, m)
                if m >= 1:
                    dispatch_low(0, m - 1)
            dispatch_low(0, TT - 1)
            with pool.Fori(1, CH) as n:
                softmaxes(n)

        @block.scalar
        def _(act):
            def embedding_high(i):
                for h in range(DH):
                    act.wait_ge(sem["emb_T"], DH * i + h + 1)
                    act.activation(embTh[:, h], psum[6 + h], ACT.Copy).then_inc(sem["embT_hi"], 1)

            def exp_k(i):
                for h in range(DH):
                    act.wait_ge(sem["qkv_done"], QKV * i + h + 1)
                    act.wait_ge(sem["kb_ready"], i + 1)
                    act.activation(ekT[:, h], psum[h], ACT.Exp, bias=kb[:, h:h + 1]).then_inc(sem["ek_ready"], 1)

            def exp_q(i):
                for h in range(DH):
                    act.wait_ge(sem["qkv_done"], QKV * i + 2 * DH + h + 1)
                    if reached(i):
                        act.wait_ge(sem["den_read"], DH * i)
                    act.activation(eq[:, h], psum[4 + h], ACT.Exp, bias=nbq[:, h:h + 1],
                                   scale=-1.0).then_inc(sem["eq_ready"], 1)

            def exp_w():
                act.wait_ge(sem["wmax_ready"], 1)
                for t in range(TT):
                    act.activation(pos[:, t], pos[:, t], ACT.Exp, bias=nwmax[:, t:t + 1]).then_inc(sem["ew_ready"], 1)

            def ew_high():
                for j in range(TT):
                    act.wait_ge(sem["ew_T"], j + 1)
                    act.activation(ewTh[:, j], psum[6 + j % 2], ACT.Copy).then_inc(sem["ewT_hi"], 1)

            def ek_high(i):
                for j in range(TT):
                    act.wait_ge(sem["ek_T"], TT * i + j + 1)
                    act.activation(EKh[:, j], psum[EK_BANKS[j]], ACT.Copy).then_inc(sem["EK_hi"], 1)

            def a_high(j):
                for h in range(DH):
                    act.wait_ge(sem["a_T"], DH * j + h + 1)
                    act.activation(aTh[:, h], psum[4 + h], ACT.Copy).then_inc(sem["aT_hi"], 1)

            def hidden(j):
                for m in range(HT):
                    act.wait_ge(sem["ffn1_done"], HT * j + m + 1)
                    act.activation(hT[:, m], psum[4 + m % 2], ACT.Relu,
                                   bias=b1c[:, m:m + 1]).then_inc(sem["h_ready"], 1)

            def z_high(j):
                act.wait_ge(sem["z_ready"], TT * (j + 1))
                act.activation(z16h[:, j], z_sb[:], ACT.Copy, scale=Z_SCALE).then_inc(sem["z16_hi"], 1)
                for h in range(DH):
                    act.wait_ge(sem["z_T"], DH * j + h + 1)
                    act.activation(zTh[:, h, j], psum[6 + h], ACT.Copy).then_inc(sem["zT_hi"], 1)

            def phi_high(n):
                act.wait_ge(sem["phi_in"], 16 * (n + 1))
                if reached(n, 2):
                    act.wait_ge(sem["l_full"], TT * (n - 1))
                for h in range(DH):
                    ins = act.activation(phih[:, n % 2, h].rearrange("p (g s e) -> p g e s", g=SUB, s=PE_),
                                         phi_by_slot(h), ACT.Copy)
                ins.then_inc(sem["phi_hi"], 1)

            act.wait_ge(sem["wqkv_in"], 48)
            act.activation(wqkvh[:], wqkv_raw[:], ACT.Copy).then_inc(sem["wqkv_hi"], 1)
            embedding_high(0)
            act.wait_ge(sem["nbq_ready"], 1)
            exp_w()
            exp_k(0)
            ew_high()
            exp_q(0)
            ek_high(0)
            embedding_high(1)
            act.wait_ge(sem["w1_in"], 16)
            act.activation(w1h[:], w1_raw[:], ACT.Copy).then_inc(sem["w1_hi"], 1)

            exp_k(1)
            exp_q(1)
            ek_high(1)
            a_high(0)
            hidden(0)
            embedding_high(2)
            with act.Fori(2, B) as i:
                exp_k(i)
                exp_q(i)
                ek_high(i)
                a_high(i - 1)
                hidden(i - 1)
                embedding_high(i + 1)
                z_high(i - 2)
            a_high(B - 1)
            hidden(B - 1)
            phi_high(0)
            z_high(B - 2)
            z_high(B - 1)

            def dispatch_high(n, m):
                act.wait_ge(sem["d_ready"], TT * n + m + 1)
                if reached(n):
                    act.wait_ge(sem["slots_done"], B * n)
                act.activation(disph[:, m], ed[:, m], ACT.Copy).then_inc(sem["disp_hi"], 1)

            def softmaxes(n, m):
                L = logits_ps[m % 2]
                act.wait_ge(sem["sub_ready"], TT * n + m + 1)
                act.activation(ed[:, m], ed[:, m], ACT.Exp).then_inc(sem["e_ready"], 1)
                act.wait_ge(sem["nmax_ready"], TT * n + m + 1)
                if reached(n):
                    act.wait_ge(sem["comb_T"], SUB * (TT * (n - 1) + m + 1))
                if reached(n):
                    act.wait_ge(sem["s_ready"], TT * (n - 1) + m + 1)
                for b in range(B):
                    ins = act.activation(e2[:, m, b], L[:, b], ACT.Exp, bias=nRn[:, m, b:b + 1],
                                         accum_out=csum[:, m, b:b + 1])
                ins.then_inc(sem["e2_ready"], 1)
                if reached(n, 2):
                    act.wait_ge(sem["acc_added"], 2 * (TT * (n - 2) + m + 1))
                act.activation(alpha[:, n % 2, m], dR[:, m], ACT.Exp).then_inc(sem["alpha_ready"], 1)

            def slots_out(c, b):
                act.wait_ge(sem["slots_done"], B * c + b + 1)
                if reached(c):
                    act.wait_ge(sem["y_done"], (CE // 2) * c)
                for h in range(DH):
                    ins = act.activation(slotsT[:, h, :, b, :].rearrange("p (g e) s -> p g s e", g=SUB),
                                         psum[4 + b % 2][:, h * CS:(h + 1) * CS].rearrange(
                                             "p (g s e) -> p g s e", g=SUB, s=PE_),
                                         ACT.Copy, scale=1.0 / (Z_SCALE * D_SCALE))
                ins.then_inc(sem["slotsT_ready"], 1)

            def combine_out(n, m):
                for k in range(SUB):
                    act.wait_ge(sem["comb_T"], SUB * (TT * n + m) + k + 1)
                    act.activation(combT[:, k, :, m, :], psum[COMB_BANKS[m] + k].rearrange("p (b t) -> p b t", b=B),
                                   ACT.Copy).then_inc(sem["combT_ready"], 1)

            phi_high(1)
            softmaxes(0, 0)
            softmaxes(0, 1)
            dispatch_high(0, 0)
            combine_out(0, 0)
            softmaxes(0, 2)
            dispatch_high(0, 1)
            combine_out(0, 1)
            softmaxes(0, 3)
            dispatch_high(0, 2)
            dispatch_high(0, 3)
            softmaxes(1, 0)

            def step(c, n=None, after=None):
                slots_out(c, 0)
                combine_out(c, 2)
                if after is not None:
                    phi_high(after)
                if n is not None:
                    softmaxes(n, 1)
                slots_out(c, 1)
                slots_out(c, 2)
                slots_out(c, 3)
                combine_out(c, 3)
                if n is None:
                    return
                dispatch_high(n, 0)
                dispatch_high(n, 1)
                softmaxes(n, 2)
                softmaxes(n, 3)
                combine_out(n, 0)
                combine_out(n, 1)
                dispatch_high(n, 2)
                dispatch_high(n, 3)
                if after is not None:
                    softmaxes(after, 0)

            step(0, 1, 2)
            with act.Fori(1, CH - 2) as c:
                step(c, c + 1, c + 2)
            step(CH - 2, CH - 1)
            step(CH - 1)

        @block.vector
        def _(dve):
            def row(i):
                return rows[:, i:i + 1].broadcast_to([P, TT, D])

            def statistics(n, src, source, count, per_tile=0):
                for t in range(TT):
                    if t == 0 or per_tile:
                        dve.wait_ge(source, count + per_tile * t)
                    dve.bn_stats(st[n][:, t], src[:, t]).then_inc(dve_order, 1)
                    k = order.step()
                dve.wait_ge(dve_order, order.value(k))
                dve.memset(ve[n][:], EPS).then_inc(dve_order, 1)
                order.step()
                for t in range(TT):
                    dve.bn_aggr(mv[n][:, t], st[n][:, t]).then_inc(dve_order, 1)
                    last = order.step()
                dve.wait_ge(dve_order, order.value(last))
                dve.tensor_tensor(ve[n][:], mv[n][:, :, 1], ve[n][:], ALU.add).then_inc(var_ready[n], 1)

            def normalise(n, count, src, dst):
                dve.wait_ge(rstd_ready[n], count)
                for t in range(TT):
                    ins = dve.tensor_scalar(dst[:, t], src[:, t], mv[n][:, t, 0:1], rstd[n][:, t:t + 1],
                                            ALU.subtract, ALU.mult)
                    ins.then_inc(dve_order, 1)
                    k = order.step()
                return k

            def embedding_stats(made):
                statistics("x", xf, sem["x_in"], 16 * (made + 1))

            def embedding(made):
                if reached(made):
                    dve.wait_ge(sem["emb_T"], DH * made)
                    dve.wait_ge(sem["embb_made"], made)
                k = normalise("x", made + 1, xf, emb)
                dve.wait_ge(sem["ctx_arrived"], 16 * (made + 1))
                dve.wait_ge(dve_order, order.value(k))
                dve.tensor_tensor(emb[:], emb[:], ctxf[:], ALU.add).then_inc(sem["emb_ready"], 1)

            def embedding_low(i):
                for h in range(DH):
                    dve.wait_ge(sem["embT_hi"], DH * i + h + 1)
                    dve.tensor_tensor(embTl[:, h], psum[6 + h], embTh[:, h].bitcast(F32),
                                      ALU.subtract).then_inc(sem["embT_lo"], 1)

            def embedding_bias(i):
                dve.wait_ge(sem["emb_ready"], i + 1)
                dve.tensor_tensor(embb[:], emb[:], row(0), ALU.add).then_inc(sem["embb_made"], 1)

            def k_maxima(i):
                for h in range(DH):
                    dve.wait_ge(sem["qkv_done"], QKV * i + h + 1)
                    dve.tensor_reduce(km[:, h:h + 1], psum[h], AX_X, ALU.max).then_inc(dve_order, 1)
                    k = order.step()
                dve.wait_ge(dve_order, order.value(k))
                dve.tensor_tensor(kmb[:], km[:], cols[:, 1], ALU.add).then_inc(dve_order, 1)
                k = order.step()
                dve.wait_ge(dve_order, order.value(k))
                dve.tensor_tensor(kb[:], cols[:, 1], kmb[:], ALU.subtract).then_inc(sem["kb_ready"], 1)

            def ek_times_v(i):
                for h in range(DH):
                    dve.wait_ge(sem["qkv_done"], QKV * i + DH + h + 1)
                    dve.wait_ge(sem["ek_ready"], DH * i + h + 1)
                    dve.scalar_tensor_tensor(ekvT[:, h], psum[2 + h], cols[:, 2, h:h + 1], ekT[:, h],
                                             ALU.add, ALU.mult).then_inc(sem["ekv_ready"], 1)

            def ek_low(i):
                for j in range(TT):
                    dve.wait_ge(sem["EK_hi"], TT * i + j + 1)
                    dve.tensor_tensor(EKl[:, j], psum[EK_BANKS[j]], EKh[:, j].bitcast(F32),
                                      ALU.subtract).then_inc(sem["EK_lo"], 1)

            def gate(i, h):
                bank_den, bank_num = SUMS_BANKS[h]
                dve.wait_ge(sem["sums_done"], 2 * (DH * i + h) + 1)
                dve.wait_ge(sem["eq_ready"], DH * i + h + 1)
                dve.scalar_tensor_tensor(yT[:, h], eq[:, h], 1.0, psum[bank_den], ALU.add,
                                         ALU.mult).then_inc(sem["den_read"], 1)
                dve.wait_ge(sem["den_read"], DH * i + h + 1)
                dve.reciprocal(yT[:, h], yT[:, h]).then_inc(dve_order, 1)
                k = order.step()
                dve.wait_ge(sem["sums_done"], 2 * (DH * i + h) + 2)
                dve.wait_ge(dve_order, order.value(k))
                dve.tensor_tensor(yT[:, h], psum[bank_num], yT[:, h], ALU.mult).then_inc(sem["y_ready"], 1)

            def attention_sum(j):
                dve.wait_ge(sem["embb_made"], j + 1)
                for t in range(TT):
                    dve.wait_ge(sem["attn_done"], TT * j + t + 1)
                    dve.tensor_tensor(a_sb[:, t], psum[6 + t % 2][:, 0:D], embb[:, t],
                                      ALU.add).then_inc(sem["s_added"], 1)
                statistics("a", a_sb, sem["s_added"], TT * j + 1, 1)

            def scale_gamma(n, src, t):
                dve.scalar_tensor_tensor(src[:, t], src[:, t], mv[n][:, t, 0:1], rows[:, 1],
                                         ALU.subtract, ALU.mult).then_inc(dve_order, 1)
                return order.step()

            def scale_add(n, src, t, summand):
                return dve.scalar_tensor_tensor(src[:, t], src[:, t], rstd[n][:, t:t + 1], summand, ALU.mult, ALU.add)

            def attention_norm(j):
                for t in range(TT):
                    k = scale_gamma("a", a_sb, t)
                dve.wait_ge(rstd_ready["a"], j + 1)
                dve.wait_ge(dve_order, order.value(k))
                for t in range(TT):
                    ins = scale_add("a", a_sb, t, rows[:, 2])
                ins.then_inc(sem["a_ready"], 1)

            def attention_bias(j):
                dve.wait_ge(sem["a_ready"], j + 1)
                if reached(j):
                    dve.wait_ge(sem["z_ready"], TT * j)
                dve.wait_ge(sem["xb_in"], 16 * (j + 1))
                dve.tensor_tensor(ab2[:], a_sb[:], row(3), ALU.add).then_inc(dve_order, 1)
                return order.step()

            def a_low(j):
                for h in range(DH):
                    dve.wait_ge(sem["aT_hi"], DH * j + h + 1)
                    dve.tensor_tensor(aTl[:, h], psum[4 + h], aTh[:, h].bitcast(F32),
                                      ALU.subtract).then_inc(sem["aT_lo"], 1)

            def ffn_sum(j, t, k_ab2=None):
                if k_ab2 is not None:
                    dve.wait_ge(dve_order, order.value(k_ab2))
                dve.wait_ge(sem["ffn2_done"], TT * j + t + 1)
                dve.tensor_tensor(ab2[:, t], psum[4 + t % 2][:, 0:D], ab2[:, t], ALU.add).then_inc(sem["s2_added"], 1)

            def block_output(j):
                statistics("f", ab2, sem["s2_added"], TT * j + 1, 1)
                for t in range(TT):
                    k = scale_gamma("f", ab2, t)
                dve.wait_ge(sem["xb_ready"], j + 1)
                dve.wait_ge(rstd_ready["f"], j + 1)
                dve.wait_ge(dve_order, order.value(k))
                for t in range(TT):
                    ins = scale_add("f", ab2, t, xb[:, t])
                ins.then_inc(sem["x1_ready"], 1)
                statistics("z", ab2, sem["x1_ready"], j + 1)
                dve.wait_ge(rstd_ready["z"], j + 1)
                for t in range(TT):
                    dve.tensor_scalar(z_sb[:, t], ab2[:, t], mv["z"][:, t, 0:1], rstd["z"][:, t:t + 1],
                                      ALU.subtract, ALU.mult).then_inc(sem["z_ready"], 1)

            def statistics_tile(n, src, source, count, t):
                dve.wait_ge(source, count)
                dve.bn_stats(st[n][:, t], src[:, t]).then_inc(dve_order, 1)
                k = order.step()
                dve.wait_ge(dve_order, order.value(k))
                dve.memset(ve[n][:, t:t + 1], EPS).then_inc(dve_order, 1)
                order.step()
                dve.bn_aggr(mv[n][:, t], st[n][:, t]).then_inc(dve_order, 1)
                k = order.step()
                dve.wait_ge(dve_order, order.value(k))
                dve.tensor_tensor(ve[n][:, t:t + 1], mv[n][:, t, 1:2], ve[n][:, t:t + 1],
                                  ALU.add).then_inc(var_ready[n], 1)

            def last_tile(n, t):
                j = B - 1
                if n == "sum":
                    ffn_sum(j, t)
                elif n == "f":
                    statistics_tile("f", ab2, sem["s2_added"], TT * j + t + 1, t)
                elif n == "z":
                    k = scale_gamma("f", ab2, t)
                    dve.wait_ge(rstd_ready["f"], B + t)
                    dve.wait_ge(dve_order, order.value(k))
                    scale_add("f", ab2, t, xb[:, t]).then_inc(sem["x1_ready"], 1)
                    statistics_tile("z", ab2, sem["x1_ready"], j + t + 1, t)
                else:
                    dve.wait_ge(rstd_ready["z"], B + t)
                    dve.tensor_scalar(z_sb[:, t], ab2[:, t], mv["z"][:, t, 0:1], rstd["z"][:, t:t + 1],
                                      ALU.subtract, ALU.mult).then_inc(sem["z_ready"], 1)

            def z_low(j):
                dve.wait_ge(sem["z16_hi"], j + 1)
                dve.scalar_tensor_tensor(z16l[:, j], z_sb[:], Z_SCALE, z16h[:, j],
                                         ALU.mult, ALU.subtract).then_inc(sem["z16_lo"], 1)
                for h in range(DH):
                    dve.wait_ge(sem["zT_hi"], DH * j + h + 1)
                    dve.tensor_tensor(zTl[:, h, j], psum[6 + h], zTh[:, h, j].bitcast(F32),
                                      ALU.subtract).then_inc(sem["zT_lo"], 1)

            def phi_low(n):
                dve.wait_ge(sem["phi_hi"], n + 1)
                for h in range(DH):
                    high, low = (t[:, n % 2, h].rearrange("p (g s e) -> p g e s", g=SUB, s=PE_) for t in (phih, phil))
                    ins = dve.tensor_tensor(low, phi_by_slot(h), high.bitcast(F32), ALU.subtract)
                ins.then_inc(sem["phi_lo"], 1)

            order = Order(0)
            embedding_stats(0)
            embedding(0)
            dve.wait_ge(sem["wqkv_hi"], 1)
            dve.tensor_tensor(wqkvl[:], wqkv_raw[:], wqkvh[:].bitcast(F32), ALU.subtract).then_inc(sem["wqkv_lo"], 1)
            dve.wait_ge(sem["vectors_in"], 16 * 8)
            dve.tensor_scalar(nbq[:], cols[:, 0], -1.0, None, ALU.mult).then_inc(sem["nbq_ready"], 1)
            embedding_low(0)
            dve.wait_ge(sem["band_masked"], 1)
            dve.tensor_reduce(wmax[:], pos[:], AX_X, ALU.max).then_inc(dve_order, 1)
            k = order.step()
            dve.wait_ge(dve_order, order.value(k))
            dve.tensor_scalar(nwmax[:], wmax[:], -1.0, None, ALU.mult).then_inc(sem["wmax_ready"], 1)
            embedding_bias(0)
            k_maxima(0)
            ek_times_v(0)
            for j in range(TT):
                dve.wait_ge(sem["ewT_hi"], j + 1)
                dve.tensor_tensor(ewTl[:, j], psum[6 + j % 2], ewTh[:, j].bitcast(F32),
                                  ALU.subtract).then_inc(sem["ewT_lo"], 1)
            ek_low(0)
            embedding_stats(1)
            embedding(1)
            embedding_low(1)
            gate(0, 0)
            gate(0, 1)
            assert order.k == STEPS_A0, order.k

            def turn(i, end=True):
                attention_sum(i - 1)
                k_maxima(i)
                embedding_bias(i)
                ek_times_v(i)
                ek_low(i)
                attention_norm(i - 1)
                embedding_stats(i + 1)
                embedding(i + 1)
                a_low(i - 1)
                if end:
                    block_output(i - 2)
                embedding_low(i + 1)
                gate(i, 0)
                k_ab2 = attention_bias(i - 1)
                ffn_sum(i - 1, 0, k_ab2)
                if end:
                    z_low(i - 2)
                ffn_sum(i - 1, 1)
                gate(i, 1)
                ffn_sum(i - 1, 2)
                ffn_sum(i - 1, 3)

            order = Order(STEPS_A0)
            turn(1, end=False)
            assert order.k == STEPS_A1, order.k
            with dve.Fori(2, B) as i:
                order = Order(STEPS_A0 + STEPS_A1 + STEPS_A * (i - 2))
                turn(i)
                assert order.k == STEPS_A, order.k
            order = Order(STEPS_A0 + STEPS_A1 + STEPS_A * (B - 2))
            attention_sum(B - 1)
            attention_norm(B - 1)
            a_low(B - 1)
            block_output(B - 2)
            k_ab2 = attention_bias(B - 1)
            dve.wait_ge(dve_order, order.value(k_ab2))
            dve.wait_ge(sem["xb_ready"], B)
            for at, (n, t) in enumerate(LAST_TILES):
                if at == 2:
                    z_low(B - 2)
                    phi_low(0)
                last_tile(n, t)
            z_low(B - 1)
            assert order.k == STEPS_A2, order.k

            dve.wait_ge(sem["x1_spilled"], 16 * B)
            dve.wait_ge(sem["z16_lo"], B)
            dve.wait_ge(sem["zT_lo"], DH * B)
            dve.memset(S[:], 0.0).then_inc(sem["zeroed"], 1)
            dve.memset(nR[:], -LOWEST).then_inc(sem["zeroed"], 1)
            dve.wait_ge(sem["zeroed"], 2)

            def maxima(n, m):
                L = logits_ps[m % 2]
                dve.wait_ge(sem["l_full"], TT * n + m + 1)
                dve.tensor_reduce(cmax[:, m], L, AX_X, ALU.max).then_inc(dve_order, 1)
                k_c = order.step()
                dve.tensor_reduce(mx[:], L.rearrange("p b n -> p n b"), AX_X, ALU.max).then_inc(dve_order, 1)
                k_m = order.step()
                dve.wait_ge(dve_order, order.value(k_c))
                dve.scalar_tensor_tensor(nRn[:, m], cmax[:, m], -1.0, nR[:, m], ALU.mult,
                                         ALU.min).then_inc(dve_order, 1)
                k_r = order.step()
                if reached(n):
                    dve.wait_ge(sem["disp_lo"], TT * (n - 1) + m + 1)
                dve.wait_ge(dve_order, order.value(k_m))
                dve.tensor_tensor(ed[:, m], L, mx[:].rearrange("p (a n) -> p a n", a=1).broadcast_to([P, B, CS]),
                                  ALU.subtract).then_inc(sem["sub_ready"], 1)
                dve.wait_ge(dve_order, order.value(k_r))
                dve.tensor_tensor(dR[:, m], nRn[:, m], nR[:, m], ALU.subtract).then_inc(sem["nmax_ready"], 1)
                dve.wait_ge(sem["nmax_ready"], TT * n + m + 1)
                dve.tensor_copy(nR[:, m], nRn[:, m]).then_inc(dve_order, 1)
                order.step()

            def dispatch(n, m):
                e = ed[:, m]
                dve.wait_ge(sem["ssum_ready"], TT * n + m + 1)
                dve.reciprocal(ssum[:, m % 2], ssum[:, m % 2]).then_inc(dve_order, 1)
                k = order.step()
                dve.wait_ge(dve_order, order.value(k))
                dve.scalar_tensor_tensor(e, e, D_SCALE, ssum[:, m % 2:m % 2 + 1].broadcast_to([P, B, CS]),
                                         ALU.mult, ALU.mult).then_inc(sem["d_ready"], 1)

            def add_bias(c, j):
                if j == 0:
                    dve.wait_ge(sem["eb_in"], 16 * (c + 1))
                    if reached(c):
                        for k in range(2):
                            dve.wait_ge(y_moved[k], 16 * SUB * (B // 2) * c)
                dve.wait_ge(sem["y_done"], (CE // 2) * c + j + 1)
                bank = psum[4 + j].rearrange("p (n e) -> p n e", n=2)
                dve.tensor_tensor(y_sb[:, 2 * j:2 * j + 2], bank, ebb[:, 2 * j:2 * j + 2],
                                  ALU.add).then_inc(sem["y_ready_b"], 1)

            def accumulate(c, m):
                dve.wait_ge(sem["alpha_ready"], TT * c + m + 1)
                for k in range(2):
                    dve.wait_ge(sem["out_done"], 2 * (TT * c + m) + k + 1)
                    for q in range(2):
                        b = 2 * k + q
                        ins = dve.scalar_tensor_tensor(acc[:, b, m], acc[:, b, m], alpha[:, c % 2, m, b:b + 1],
                                                       psum[OUT_BANKS[m] + k][:, q * D:(q + 1) * D],
                                                       ALU.mult, ALU.add)
                    ins.then_inc(sem["acc_added"], 1)

            BASE_B = STEPS_A0 + STEPS_A1 + STEPS_A * (B - 2) + STEPS_A2
            order = Order(BASE_B)
            maxima(0, 0)
            phi_low(1)
            for m in range(1, TT):
                maxima(0, m)
                dispatch(0, m - 1)
            dispatch(0, TT - 1)
            maxima(1, 0)
            assert order.k == STEPS_B0, order.k

            def step(c, n=None, after=None):
                if n is None:
                    for j in range(CE // 2):
                        add_bias(c, j)
                    dve.wait_ge(sem["s_ready"], TT * CH)
                    dve.reciprocal(rS[:], S[:]).then_inc(sem["rS_ready"], 1)
                    dve.wait_ge(sem["rS_ready"], 1)
                    for m in range(TT):
                        accumulate(c, m)
                        dve.wait_ge(sem["acc_added"], 2 * (TT * c + m + 1))
                        if m == 0:
                            dve.wait_ge(sem["x1_back"], 16 * B)
                        for b in range(B):
                            ins = dve.scalar_tensor_tensor(acc[:, b, m], acc[:, b, m], rS[:, m, b:b + 1],
                                                           x1_view[:, b, m], ALU.mult, ALU.add)
                        ins.then_inc(sem["out_ready"], 1)
                    return
                maxima(n, 1)
                dispatch(n, 0)
                if after is not None:
                    phi_low(after)
                dispatch(n, 1)
                for j in range(CE // 2):
                    add_bias(c, j)
                maxima(n, 2)
                maxima(n, 3)
                accumulate(c, 0)
                accumulate(c, 1)
                dispatch(n, 2)
                dispatch(n, 3)
                accumulate(c, 2)
                if after is not None:
                    maxima(after, 0)
                accumulate(c, 3)

            order = Order(BASE_B + STEPS_B0)
            dve.wait_ge(sem["acc_zeroed"], 1)
            step(0, 1, 2)
            assert order.k == STEPS_B, order.k
            with dve.Fori(1, CH - 2) as c:
                order = Order(BASE_B + STEPS_B0 + STEPS_B * c)
                step(c, c + 1, c + 2)
                assert order.k == STEPS_B, order.k
            order = Order(BASE_B + STEPS_B0 + STEPS_B * (CH - 2))
            step(CH - 2, CH - 1)
            step(CH - 1)

        @block.tensor
        def _(pe):
            def split3(out_ap, Lh, Ll, Rh, Rl, start, stop):
                pe.matmul(out_ap, Lh, Rh, start=start, stop=False)
                pe.matmul(out_ap, Lh, Rl, start=False, stop=False)
                return pe.matmul(out_ap, Ll, Rh, start=False, stop=stop)

            def transposes(bank, sources):
                for q, src in enumerate(sources):
                    mm = pe.transpose(bank[:, q * P:(q + 1) * P], src, ident[:])
                return mm

            def t_emb(i):
                pe.wait_ge(sem["emb_ready"], i + 1)
                for h in range(DH):
                    if reached(i):
                        pe.wait_ge(sem["EK_lo"], TT * (i - 1) + 1 + h)
                    transposes(psum[6 + h], [emb[:, t, h * P:(h + 1) * P] for t in range(TT)]).then_inc(sem["emb_T"], 1)

            def qkv(i, turns=(0, 1, 2)):
                pe.wait_ge(sem["embT_lo"], DH * (i + 1))
                for turn in turns:
                    w = (1, 2, 0)[turn]
                    for e in range(DH):
                        bank = psum[2 * turn + e]
                        if turn == 2 and reached(i, 2):
                            pe.wait_ge(sem["s2_added"], TT * (i - 2) + 3 + e)
                        for h in range(DH):
                            mm = split3(bank, wqkvh[:, w, h, e * P:(e + 1) * P], wqkvl[:, w, h, e * P:(e + 1) * P],
                                        embTh[:, h], embTl[:, h], h == 0, h == DH - 1)
                        mm.then_inc(sem["qkv_done"], 1)

            def t_ek(i):
                pe.wait_ge(sem["ekv_ready"], DH * (i + 1))
                for j in range(TT):
                    if j < 2 and reached(i):
                        pe.wait_ge(sem["s_added"], TT * (i - 1) + 3 + j)
                    elif j < 2:
                        pe.wait_ge(sem["ewT_lo"], TT - 1 + j)
                    transposes(psum[EK_BANKS[j]], [src[:, h, j * P:(j + 1) * P] for src in (ekT, ekvT)
                                                 for h in range(DH)]).then_inc(sem["ek_T"], 1)

            def aft(i, h):
                for kind in range(2):
                    bank = psum[SUMS_BANKS[h][kind]]
                    if h == 0:
                        pe.wait_ge(sem["ekv_ready"], DH * i + kind + 1)
                    else:
                        pe.wait_ge(sem["EK_lo"], TT * (i + 1))
                    c0 = kind * D + h * P
                    for j in range(TT):
                        if h == 0 and kind == 0:
                            pe.wait_ge(sem["EK_lo"], TT * i + j + 1)
                        mm = split3(bank, EKh[:, j, c0:c0 + P], EKl[:, j, c0:c0 + P], ewTh[:, j], ewTl[:, j],
                                    j == 0, j == TT - 1)
                    mm.then_inc(sem["sums_done"], 1)

            def attention(j):
                pe.wait_ge(sem["y_ready"], DH * (j + 1))
                for t in range(TT):
                    bank = psum[6 + t % 2]
                    if t >= 2:
                        pe.wait_ge(sem["s_added"], TT * j + t - 1)
                    for h in range(DH):
                        mm = pe.matmul(bank[:, 0:D], yT[:, h, t * P:(t + 1) * P], wo_sb[:, h],
                                       start=(h == 0), stop=(h == DH - 1))
                    mm.then_inc(sem["attn_done"], 1)

            def t_a(j):
                pe.wait_ge(sem["a_ready"], j + 1)
                for h in range(DH):
                    if reached(j + 1) and not (isinstance(j, int) and j == B - 1):
                        pe.wait_ge(sem["eq_ready"], DH * (j + 1) + h + 1)
                    transposes(psum[4 + h], [a_sb[:, t, h * P:(h + 1) * P] for t in range(TT)]).then_inc(sem["a_T"], 1)

            def ffn1(j):
                pe.wait_ge(sem["aT_lo"], DH * (j + 1))
                for m in range(HT):
                    bank = psum[4 + m % 2]
                    if m >= 2:
                        pe.wait_ge(sem["h_ready"], HT * j + m - 1)
                    for h in range(DH):
                        mm = split3(bank, w1h[:, h, m * P:(m + 1) * P], w1l[:, h, m * P:(m + 1) * P],
                                    aTh[:, h], aTl[:, h], h == 0, h == DH - 1)
                    mm.then_inc(sem["ffn1_done"], 1)

            def ffn2(j, tiles):
                for t in tiles:
                    bank = psum[4 + t % 2]
                    if t >= 2:
                        pe.wait_ge(sem["s2_added"], TT * j + t - 1)
                    else:
                        pe.wait_ge(sem["h_ready"], HT * j + HT - 1 + t)
                    for m in range(HT):
                        if t == 0:
                            pe.wait_ge(sem["h_ready"], HT * j + m + 1)
                        mm = pe.matmul(bank[:, 0:D], hT[:, m, t * P:(t + 1) * P], w2_sb[:, m],
                                       start=(m == 0), stop=(m == HT - 1))
                    mm.then_inc(sem["ffn2_done"], 1)

            def t_z(j):
                pe.wait_ge(sem["z_ready"], TT * (j + 1))
                for h in range(DH):
                    if isinstance(j, int) and j == B - 1:
                        pe.wait_ge(sem["zT_lo"], DH * (j - 1) + h + 1)
                    elif isinstance(j, int) and j == B - 2:
                        pe.wait_ge(sem["s_added"], TT * (B - 1) + 3 + h)
                    else:
                        pe.wait_ge(sem["embT_lo"], DH * (j + 3) + h + 1)
                    transposes(psum[6 + h], [z_sb[:, t, h * P:(h + 1) * P] for t in range(TT)]).then_inc(sem["z_T"], 1)

            def logits(n, m, batches=range(B)):
                if m == 0:
                    pe.wait_ge(sem["phi_lo"], n + 1)
                if reached(n) or m >= 2:
                    pe.wait_ge(sem["e2_ready"], TT * n + m - 1)
                for b in batches:
                    for h in range(DH):
                        mm = split3(logits_ps[m % 2][:, b],
                                    zTh[:, h, b, m * P:(m + 1) * P], zTl[:, h, b, m * P:(m + 1) * P],
                                    phih[:, n % 2, h], phil[:, n % 2, h], h == 0, h == DH - 1)
                if B - 1 in batches:
                    mm.then_inc(sem["l_full"], 1)

            pe.wait_ge(sem["ident_made"], 1)
            t_emb(0)
            pe.wait_ge(sem["wqkv_lo"], 1)
            qkv(0, (0, 1))
            pe.wait_ge(sem["embT_lo"], DH)
            pe.wait_ge(sem["ew_ready"], TT)
            for j in range(TT):
                if j >= 2:
                    pe.wait_ge(sem["ewT_lo"], j - 1)
                for t in range(TT):
                    mm = pe.transpose(psum[6 + j % 2][:, t * P:(t + 1) * P], pos[:, t, j * P:(j + 1) * P], ident[:])
                mm.then_inc(sem["ew_T"], 1)
            qkv(0, (2,))
            t_ek(0)
            pe.wait_ge(sem["ewT_lo"], TT)
            aft(0, 0)
            t_emb(1)
            aft(0, 1)
            pe.wait_ge(sem["wo_w2_in"], 32)

            def turn(i, end=True):
                attention(i - 1)
                qkv(i)
                t_ek(i)
                aft(i, 0)
                t_a(i - 1)
                aft(i, 1)
                if not end:
                    pe.wait_ge(sem["w1_lo"], 1)
                ffn1(i - 1)
                t_emb(i + 1)
                ffn2(i - 1, [0])
                if end:
                    t_z(i - 2)
                ffn2(i - 1, range(1, TT))

            turn(1, end=False)
            with pe.Fori(2, B) as i:
                turn(i)
            attention(B - 1)
            t_a(B - 1)
            ffn1(B - 1)
            ffn2(B - 1, [0])
            t_z(B - 2)
            ffn2(B - 1, range(1, TT))
            pe.wait_ge(sem["zT_lo"], DH * (B - 1))
            for m in range(2):
                logits(0, m, range(B - 1))
            t_z(B - 1)

            def t_combine(n, m):
                pe.wait_ge(sem["e2_ready"], TT * n + m + 1)
                for k in range(SUB):
                    if m == 3:
                        pe.wait_ge(sem["combT_ready"], SUB * (TT * n + 2) + k + 1)
                    elif m == 2 and reached(n):
                        pe.wait_ge(sem["acc_added"], 2 * (TT * (n - 1) + 3) + k + 1)
                    elif m == 2:
                        pe.wait_ge(sem["combT_ready"], SUB + k + 1)
                    elif reached(n):
                        pe.wait_ge(sem["acc_added"], 2 * (TT * (n - 1) + m) + k + 1)
                    transposes(psum[COMB_BANKS[m] + k],
                               [e2[:, m, b, k * P:(k + 1) * P] for b in range(B)]).then_inc(sem["comb_T"], 1)

            def slots(c, b):
                if b == 0:
                    pe.wait_ge(sem["disp_lo"], TT * (c + 1))
                bank = psum[4 + b % 2]
                if b >= 2:
                    pe.wait_ge(sem["slotsT_ready"], B * c + b - 1)
                elif reached(c):
                    pe.wait_ge(sem["acc_added"], 2 * (TT * (c - 1) + 2) + b + 1)
                else:
                    pe.wait_ge(sem["combT_ready"], b + 1)
                for h in range(DH):
                    for m in range(TT):
                        hs = slice(h * P, (h + 1) * P)
                        mm = split3(bank[:, h * CS:(h + 1) * CS], z16h[:, b, m, hs], z16l[:, b, m, hs],
                                    disph[:, m, b], displ[:, m, b], m == 0, m == TT - 1)
                mm.then_inc(sem["slots_done"], 1)

            def experts(c):
                pe.wait_ge(sem["slotsT_ready"], B * (c + 1))
                for j in range(CE // 2):
                    bank = psum[4 + j]
                    if j >= 2:
                        pe.wait_ge(sem["combT_ready"], SUB * (TT * c + 3) + j - 1)
                    if j % 2 == 0:
                        pe.wait_ge(W_in[j // 2], 16 * (c + 1))
                    for q in range(2):
                        for h in range(DH):
                            mm = pe.matmul(bank[:, q * D:(q + 1) * D],
                                           slotsT[:, h, 2 * j + q].rearrange("p b s -> p (b s)"), Wr[:, 2 * j + q, h],
                                           start=(h == 0), stop=(h == DH - 1))
                    mm.then_inc(sem["y_done"], 1)

            def combine(c, m, n):
                if m == 0:
                    pe.wait_ge(sem["combT_ready"], SUB * TT * (c + 1))
                for k in range(2):
                    bank = psum[OUT_BANKS[m] + k]
                    if m == 0:
                        pe.wait_ge(y_moved[k], 16 * SUB * (B // 2) * (c + 1))
                        pe.wait_ge(sem["y_ready_b"], (CE // 2) * c + k + 1)
                    elif m == 1:
                        pe.wait_ge(sem["y_ready_b"], (CE // 2) * c + 2 + k + 1)
                    elif n is not None:
                        pe.wait_ge(sem["combT_ready"], SUB * (TT * n + m - 2) + k + 1)
                    else:
                        pe.wait_ge(sem["acc_added"], 2 * (TT * c + m - 2) + k + 1)
                    for q in range(2):
                        b = 2 * k + q
                        for u in range(SUB):
                            mm = pe.matmul(bank[:, q * D:(q + 1) * D], combT[:, u, b, m], y_c[:, u, b],
                                           start=(u == 0), stop=(u == SUB - 1))
                    mm.then_inc(sem["out_done"], 1)

            pe.wait_ge(sem["zT_lo"], DH * B)
            for m in range(2):
                logits(0, m, [B - 1])
            logits(0, 2)
            t_combine(0, 0)
            logits(0, 3)
            t_combine(0, 1)
            logits(1, 0)
            logits(1, 1)

            def step(c, n=None, after=None):
                slots(c, 0)
                t_combine(c, 2)
                slots(c, 1)
                slots(c, 2)
                slots(c, 3)
                t_combine(c, 3)
                experts(c)
                if n is not None:
                    logits(n, 2)
                    logits(n, 3)
                combine(c, 0, n)
                combine(c, 1, n)
                if after is not None:
                    logits(after, 0)
                if n is not None:
                    t_combine(n, 0)
                    t_combine(n, 1)
                combine(c, 2, n)
                if after is not None:
                    logits(after, 1)
                combine(c, 3, n)

            step(0, 1, 2)
            with pe.Fori(1, CH - 2) as c:
                step(c, c + 1, c + 2)
            step(CH - 2, CH - 1)
            step(CH - 1)


_INS = ["x", "ctx_1024", "L0_xattn_wq", "L0_xattn_bq", "L0_xattn_wk", "L0_xattn_bk", "L0_xattn_wv", "L0_xattn_bv",
        "L0_xattn_wo", "L0_xattn_bo", "L0_xattn_pos_bias", "L0_xattn_gamma", "L0_xattn_beta", "L0_xattn_w1",
        "L0_xattn_b1", "L0_xattn_w2", "L0_xattn_b2", "L0_ffn_phi", "L0_ffn_W", "L0_ffn_b"]
_OUTS = [((4, 512, 256), "float32")]


def kernel(**inputs):
    import numpy as _np
    import concourse.bacc as _bacc
    from concourse import mybir as _mybir
    from concourse.bass_utils import run_bass_kernel_spmd as _run

    nc = _bacc.Bacc("TRN2", target_bir_lowering=False, num_devices=1)
    arrays, args = {}, []
    for name in _INS:
        a = _np.ascontiguousarray(inputs[name])
        arrays[f"in_{name}_dram"] = a
        args.append(nc.dram_tensor(f"in_{name}_dram", a.shape, _mybir.dt.from_np(a.dtype), kind="ExternalInput").ap())
    for i, (shape, dtype) in enumerate(_OUTS):
        dt = _mybir.dt.from_np(_np.dtype(dtype))
        args.append(nc.dram_tensor(f"out_{i}_dram", shape, dt, kind="ExternalOutput").ap())
    bass_aft_soft_moe(nc, *args)
    r = _run(nc, [arrays], core_ids=[0])
    return r.results[0]["out_0_dram"]
```
